# Optimizing a Trainium2 kernel written in Bass

```python
import numpy as np
import jax
import jax.numpy as jnp

def _softmax(x, axis=-1):
    return jax.nn.softmax(x, axis=axis)

def _gelu(x):
    return jax.nn.gelu(x, approximate=True)

def _silu(x):
    return jax.nn.silu(x)

def _sigmoid(x):
    return jax.nn.sigmoid(x)

def _layernorm(x, axis=-1, eps=1e-05):
    m = jnp.mean(x, axis=axis, keepdims=True)
    v = jnp.var(x, axis=axis, keepdims=True)
    return (x - m) / jnp.sqrt(v + eps)

def _scatter_add(tgt, idx, src, axis=0):
    return tgt.at[idx].add(src)

def _segment_sum(src, seg, n):
    return jax.ops.segment_sum(src, seg, n)
kernel_name = 'mk_adj_preln_d1_adj_r2_6f2ef9'

def setup_inputs(seed: int=0):
    np.random.seed(seed)
    _w = jnp.asarray

    def _rec_inputs():
        import jax
        import jax.numpy as jnp
        _gk = jax.random.key(seed)
        x = -0.0001538 + 1 * jax.random.normal(jax.random.fold_in(_gk, 1), (16, 512, 384), jnp.float32)
        _a = jax.random.bernoulli(jax.random.fold_in(_gk, 2), 0.015625, (16, 512, 512))
        _af = _a.astype(jnp.float32)
        adj = _af
        return (x, adj)
    x, adj = _rec_inputs()

    def _L0_gnn_setup():
        import jax, jax.numpy as jnp
        import numpy as np
        LN_EPS = 1e-12

        def _digcn_forward(hidden_state, adjacency_matrix, Wl, bl, Ws, bs, Wr, br, ln_w, ln_b):
            B, S, D = hidden_state.shape
            temper = jnp.asarray(D, jnp.float32) ** 0.5
            i = jnp.arange(S)
            upper = (i[None, :] > i[:, None]).astype(hidden_state.dtype)
            lower = (i[None, :] < i[:, None]).astype(hidden_state.dtype)

            def layer(h, params):
                wl, b_l, ws, b_s, wr, b_r, g, beta = params
                u = jnp.einsum('bid,bjd->bij', h, h) / temper
                a = jax.nn.softmax(u, axis=-1)
                delta = a * adjacency_matrix
                attn = delta / (jnp.sum(delta, axis=-1, keepdims=True) + 1e-10)
                hl = h @ wl.T + b_l
                hs = h @ ws.T + b_s
                hr = h @ wr.T + b_r
                diag_a = jnp.diagonal(attn, axis1=1, axis2=2)
                ctx = jnp.einsum('bij,bjd->bid', attn * upper, hl) + diag_a[..., None] * hs + jnp.einsum('bij,bjd->bid', attn * lower, hr)
                mean = ctx.mean(-1, keepdims=True)
                var = ctx.var(-1, keepdims=True)
                o = (ctx - mean) / jnp.sqrt(var + LN_EPS) * g + beta
                return (jax.nn.relu(o), None)
            out, _ = jax.lax.scan(layer, hidden_state, (Wl, bl, Ws, bs, Wr, br, ln_w, ln_b))
            return out
        key = jax.random.key(seed)
        ks = jax.random.split(key, 6)
        B, S, D, L = (8, 512, 384, 2)
        scale = (1.0 / D) ** 0.5
        hidden_state = jax.random.normal(ks[0], (B, S, D), jnp.float32)
        adjacency_matrix = (jax.random.uniform(ks[1], (B, S, S)) < 0.05).astype(jnp.float32)
        Wl = jax.random.normal(ks[2], (L, D, D), jnp.float32) * scale
        Ws = jax.random.normal(ks[3], (L, D, D), jnp.float32) * scale
        Wr = jax.random.normal(ks[4], (L, D, D), jnp.float32) * scale
        bl = jnp.zeros((L, D), jnp.float32)
        bs = jnp.zeros((L, D), jnp.float32)
        br = jnp.zeros((L, D), jnp.float32)
        ln_w = jnp.ones((L, D), jnp.float32)
        ln_b = jnp.zeros((L, D), jnp.float32)
        return dict(hidden_state=hidden_state, adjacency_matrix=adjacency_matrix, Wl=Wl, bl=bl, Ws=Ws, bs=bs, Wr=Wr, br=br, ln_w=ln_w, ln_b=ln_b)
    _L0_gnn_all = _L0_gnn_setup()
    _L0_gnn_in = {k: v for k, v in _L0_gnn_all.items() if k in ('Wl', 'bl', 'Ws', 'bs', 'Wr', 'br', 'ln_w', 'ln_b')}
    del _L0_gnn_all
    return {'x': x, 'adj': adj, 'L0_gnn_Wl': _L0_gnn_in['Wl'], 'L0_gnn_bl': _L0_gnn_in['bl'], 'L0_gnn_Ws': _L0_gnn_in['Ws'], 'L0_gnn_bs': _L0_gnn_in['bs'], 'L0_gnn_Wr': _L0_gnn_in['Wr'], 'L0_gnn_br': _L0_gnn_in['br'], 'L0_gnn_ln_w': _L0_gnn_in['ln_w'], 'L0_gnn_ln_b': _L0_gnn_in['ln_b']}

def reference(x, adj, L0_gnn_Wl, L0_gnn_bl, L0_gnn_Ws, L0_gnn_bs, L0_gnn_Wr, L0_gnn_br, L0_gnn_ln_w, L0_gnn_ln_b):
    import jax
    import jax.numpy as jnp

    def _L0_gnn_ref(hidden_state, adjacency_matrix, Wl, bl, Ws, bs, Wr, br, ln_w, ln_b):
        import jax, jax.numpy as jnp
        import numpy as np
        LN_EPS = 1e-12

        def _digcn_forward(hidden_state, adjacency_matrix, Wl, bl, Ws, bs, Wr, br, ln_w, ln_b):
            B, S, D = hidden_state.shape
            temper = jnp.asarray(D, jnp.float32) ** 0.5
            i = jnp.arange(S)
            upper = (i[None, :] > i[:, None]).astype(hidden_state.dtype)
            lower = (i[None, :] < i[:, None]).astype(hidden_state.dtype)

            def layer(h, params):
                wl, b_l, ws, b_s, wr, b_r, g, beta = params
                u = jnp.einsum('bid,bjd->bij', h, h) / temper
                a = jax.nn.softmax(u, axis=-1)
                delta = a * adjacency_matrix
                attn = delta / (jnp.sum(delta, axis=-1, keepdims=True) + 1e-10)
                hl = h @ wl.T + b_l
                hs = h @ ws.T + b_s
                hr = h @ wr.T + b_r
                diag_a = jnp.diagonal(attn, axis1=1, axis2=2)
                ctx = jnp.einsum('bij,bjd->bid', attn * upper, hl) + diag_a[..., None] * hs + jnp.einsum('bij,bjd->bid', attn * lower, hr)
                mean = ctx.mean(-1, keepdims=True)
                var = ctx.var(-1, keepdims=True)
                o = (ctx - mean) / jnp.sqrt(var + LN_EPS) * g + beta
                return (jax.nn.relu(o), None)
            out, _ = jax.lax.scan(layer, hidden_state, (Wl, bl, Ws, bs, Wr, br, ln_w, ln_b))
            return out
        return _digcn_forward(hidden_state, adjacency_matrix, Wl, bl, Ws, bs, Wr, br, ln_w, ln_b)
    h = jnp.maximum(_layernorm(x, axis=-1), 0.0)
    x = x + _L0_gnn_ref(h, adj, L0_gnn_Wl, L0_gnn_bl, L0_gnn_Ws, L0_gnn_bs, L0_gnn_Wr, L0_gnn_br, L0_gnn_ln_w, L0_gnn_ln_b)
    return x

_drawn_inputs = setup_inputs


def setup_inputs(seed=0):
    import zlib

    import numpy as np

    out = dict(_drawn_inputs(seed))
    spreads = {'L0_gnn_bl': (0.0, 0.1),
     'L0_gnn_bs': (0.0, 0.581),
     'L0_gnn_br': (0.0, 0.1),
     'L0_gnn_ln_w': (1.0, 0.2),
     'L0_gnn_ln_b': (0.0, 0.1)}
    factors = {}
    for name, (base, spread) in spreads.items():
        noise = np.random.default_rng([zlib.crc32(name.encode()), seed]).standard_normal(out[name].shape)
        drawn = base * np.exp(spread * noise) if base else spread * noise
        out[name] = jnp.asarray(drawn.astype(out[name].dtype))
    for name, factor in factors.items():
        out[name] = (out[name] * factor).astype(out[name].dtype)
    return out
```

```python
from contextlib import ExitStack

import concourse.bass as bass
from concourse import mybir

F32 = mybir.dt.float32
F32R = mybir.dt.float32r
ALU = mybir.AluOpType
ACT = mybir.ActivationFunctionType

P = 128


def build_digcn(nc, x, adj, wl_t, bl, ws_t, bs, wr_t, br, ln_w, ln_b, out):
    n_graphs, n_rows, dim = x.shape
    layers = wl_t.shape[0]
    pairs = n_graphs // 2
    TILES = n_rows // P
    KB = dim // P
    scale = 1.0 / float(dim) ** 0.5
    STEPS = 2 * layers
    assert (TILES, layers) == (4, 2)

    def unit_p(t, proj):
        return 3 * t + proj

    def unit_t(db):
        return 3 * TILES + db

    C_ORDER = [("E", 0), ("E", 1), ("C", 0), ("E", 2), ("C", 1), ("E", 3), ("C", 2), ("C", 3)]

    def unit_e(i, t_units):
        return 3 * TILES + t_units + C_ORDER.index(("E", i))

    def unit_c(i, t_units):
        return 3 * TILES + t_units + C_ORDER.index(("C", i))

    UNITS = 3 * TILES + KB + len(C_ORDER)
    ROT = 4
    assert (UNITS * STEPS) % ROT == 0
    CREDIT = 8
    FREED0 = CREDIT + KB

    off_at = [0, 3 * P, 5 * P]

    ctx = ExitStack()
    with ctx:
        def sb(name, shape, dt=F32):
            return ctx.enter_context(nc.sbuf_tensor(name, shape, dt))

        def sem(name):
            return ctx.enter_context(nc.semaphore(name))

        ident = sb("ident", [P, P])
        tri = sb("tri", [P, 2, P])
        minus_half = sb("minus_half", [P, TILES])
        minus_one = sb("minus_one", [P, TILES])
        w_hi = sb("w_hi", [P, layers, KB, 3 * dim], F32R)
        w_lo = sb("w_lo", [P, layers, KB, 3 * dim], F32R)
        w_stage = sb("w_stage", [P, 3 * dim])
        bias = sb("bias", [P, layers, 3, dim])
        gamma = sb("gamma", [P, layers, dim])
        beta = sb("beta", [P, layers, dim])
        x_sb = [sb(f"x_{g}", [P, TILES, dim]) for g in "ab"]
        adj_sb = [sb(f"adj_{g}", [P, TILES, n_rows]) for g in "ab"]
        h = sb("h", [P, TILES, dim])
        ht_hi = sb("ht_hi", [P, 2, KB, n_rows], F32R)
        ht_lo = sb("ht_lo", [P, 2, KB, n_rows], F32R)
        u_off = sb("u_off", [P, 6 * P])
        e_sb = sb("e_sb", [P, TILES, n_rows])
        proj = sb("proj", [P, 2, 2 * dim])
        hw_hi = sb("hw_hi", [P, TILES, 2 * dim], F32R)
        hw_lo = sb("hw_lo", [P, TILES, 2 * dim], F32R)
        hs = sb("hs", [P, TILES, dim])
        et_hi = sb("et_hi", [P, 2, n_rows], F32R)
        et_lo = sb("et_lo", [P, 2, n_rows], F32R)
        dg = sb("dg", [P, 2, 2, 2, P], F32R)
        z = sb("z", [P, TILES, dim])
        diag_junk = sb("diag_junk", [P, TILES, P])
        neg_max = sb("neg_max", [P, TILES])
        z_sum = sb("z_sum", [P, TILES])
        e_sum = sb("e_sum", [P, TILES])
        e_diag = sb("e_diag", [P, TILES])
        den = sb("den", [P, TILES])
        recip = sb("recip", [P, TILES])
        recip_sq = sb("recip_sq", [P, TILES])
        neg_recip = sb("neg_recip", [P, TILES])
        stats = sb("stats", [P, TILES, 6])
        mv = sb("mv", [P, TILES, 2])
        var_eps = sb("var_eps", [P, TILES])
        rstd = sb("rstd", [P, TILES])
        ln_scale = sb("ln_scale", [P, TILES])
        neg_scale = sb("neg_scale", [P, TILES])
        ln_shift = sb("ln_shift", [P, TILES])
        x_stats = sb("x_stats", [P, TILES, 6])
        x_mv = sb("x_mv", [P, TILES, 2])
        x_var_eps = sb("x_var_eps", [P, TILES])
        x_rstd = sb("x_rstd", [P, TILES])
        x_neg_rstd = sb("x_neg_rstd", [P, TILES])
        x_shift = sb("x_shift", [P, TILES])

        u_ps = [ctx.enter_context(nc.psum_tensor(f"u_ps{t}", [P, n_rows], F32)) for t in range(TILES)]
        rot_ps = [ctx.enter_context(nc.psum_tensor(f"rot_ps{t}", [P, n_rows], F32)) for t in range(ROT)]

        u_raw = sem("u_raw")
        u_full = sem("u_full")
        unit_ready = sem("unit_ready")
        off_copied = sem("off_copied")
        exp_done = sem("exp_done")
        hw_hi_done = sem("hw_hi_done")
        hw_lo_done = sem("hw_lo_done")
        h_done = sem("h_done")
        ht_hi_done = sem("ht_hi_done")
        et_hi_done = sem("et_hi_done")
        z_done = sem("z_done")
        max_done = sem("max_done")
        masked = sem("masked")
        diag_done = sem("diag_done")
        recip_done = sem("recip_done")
        bank_freed = sem("bank_freed")
        stats_done = sem("stats_done")
        aggr_done = sem("aggr_done")
        var_done = sem("var_done")
        final_done = sem("final_done")
        dg_done = sem("dg_done")
        coef_chain = sem("coef_chain")
        gamma_done = sem("gamma_done")
        affine_done = sem("affine_done")
        x_stats_done = sem("x_stats_done")
        x_chain = sem("x_chain")
        x_loaded = [sem(f"x_loaded_{g}") for g in "ab"]
        adj_loaded = [sem(f"adj_loaded_{g}") for g in "ab"]
        out_stored = sem("out_stored")
        consts = sem("consts")
        vec_loaded = sem("vec_loaded")
        w_loaded = [sem("w_loaded_even"), sem("w_loaded_odd")]
        w_hi_done = sem("w_hi_done")
        w_lo0_done = sem("w_lo0_done")
        w_lo1_done = sem("w_lo1_done")

        XS = 2 * TILES + 1

        def bank(s, unit):
            return rot_ps[(UNITS * s + unit) % ROT]

        def value(per_step, it, s, count):
            return it * (STEPS * per_step) + (per_step * s + count)

        def ready(it, s, unit):
            return value(UNITS, it, s, KB + unit + 1)

        def freed(it, s, unit):
            return value(UNITS, it, s, FREED0 + unit + 1)

        def all_pairs(eng, body):
            if pairs > 1:
                with eng.Fori(0, pairs - 1) as it:
                    body(it, False)
            body(pairs - 1, True)

        def rows(dram, graph):
            return dram[graph].rearrange("(t p) n -> p t n", p=P)

        w_parts = [wl_t, wr_t, ws_t]
        chunks = [(layer, kb) for layer in range(layers) for kb in range(KB)]
        z_flat = z[:, :, :].rearrange("p t n -> p (t n)")
        w_stages = [w_stage[:, :], z_flat[:, 0:3 * dim]]

        block = ctx.enter_context(nc.Block())

        @block.sync
        def _(sp):
            def load_w(c):
                layer, kb = chunks[c]
                for n, part in enumerate(w_parts):
                    sp.dma_start(w_stages[c % 2][:, n * dim:(n + 1) * dim],
                                 part[layer, kb * P:(kb + 1) * P, :]).then_inc(w_loaded[c % 2], 16)

            sp.dma_start(x_sb[0][:, :, :], rows(x, 0)).then_inc(x_loaded[0], 16)
            load_w(0)
            load_w(1)
            sp.dma_start(adj_sb[0][:, :, :], rows(adj, 0)).then_inc(adj_loaded[0], 16)
            for tile, vec in ((bias[:, :, 0, :], bl), (bias[:, :, 1, :], br), (bias[:, :, 2, :], bs),
                              (gamma[:, :, :], ln_w), (beta[:, :, :], ln_b)):
                sp.dma_start(tile, vec.partition_broadcast(P)).then_inc(vec_loaded, 16)
            sp.dma_start(x_sb[1][:, :, :], rows(x, 1)).then_inc(x_loaded[1], 16)
            for c in range(2, len(chunks)):
                if c - 2 < KB:
                    sp.wait_ge(w_lo0_done, c - 1)
                else:
                    sp.wait_ge(w_lo1_done, c - 1 - KB)
                load_w(c)
            sp.dma_start(adj_sb[1][:, :, :], rows(adj, 1)).then_inc(adj_loaded[1], 16)

            def pair(it, last):
                for g in range(2):
                    s = 2 + g
                    if not last:
                        sp.wait_ge(masked, value(TILES, it, s, TILES))
                        sp.dma_start(adj_sb[g][:, :, :], rows(adj, it * 2 + (2 + g))).then_inc(adj_loaded[g], 16)
                    sp.wait_ge(final_done, it * (2 * TILES) + TILES * (g + 1))
                    sp.dma_start(rows(out, it * 2 + g), z[:, :, :]).then_inc(out_stored, 16)
                    if not last:
                        sp.dma_start(x_sb[g][:, :, :], rows(x, it * 2 + (2 + g))).then_inc(x_loaded[g], 16)

            all_pairs(sp, pair)
            sp.wait_ge(out_stored, 16 * (n_graphs + 1))

        @block.tensor
        def _(pe):
            def products(dst, pairs_of_operands, first=True, last=True):
                n = len(pairs_of_operands)
                for m, (a_hi, a_lo, b_hi, b_lo) in enumerate(pairs_of_operands):
                    pe.matmul(dst, a_hi, b_hi, start=first and m == 0, stop=False)
                    pe.matmul(dst, a_hi, b_lo, start=False, stop=False)
                    done = pe.matmul(dst, a_lo, b_hi, start=False, stop=last and m == n - 1)
                return done

            def transpose_h(s, db):
                for t in range(TILES):
                    done = pe.transpose(bank(s, unit_t(db))[:, t * P:(t + 1) * P],
                                        h[:, t, db * P:(db + 1) * P], ident[:, :])
                done.then_inc(unit_ready, 1)

            pe.wait_ge(consts, 6)
            pe.wait_ge(h_done, TILES)
            for db in range(KB):
                for t in range(TILES):
                    done = pe.transpose(rot_ps[(db - KB) % ROT][:, t * P:(t + 1) * P],
                                        h[:, t, db * P:(db + 1) * P], ident[:, :])
                done.then_inc(unit_ready, 1)
            pe.wait_ge(bank_freed, FREED0)

            def step(it, s, last):
                t_units = 0 if last and s == STEPS - 1 else KB
                cur, layer = s % 2, s // 2
                a_t = [ht_hi[:, cur], ht_lo[:, cur]]

                def project(t, n):
                    pe.wait_ge(bank_freed, freed(it, s, unit_p(t, n) - ROT))
                    lo, hi = t * P, (t + 1) * P
                    cols = slice(n * dim, (n + 1) * dim)
                    products(bank(s, unit_p(t, n))[:, 0:dim],
                             [(a_t[0][:, kb, lo:hi], a_t[1][:, kb, lo:hi],
                               w_hi[:, layer, kb, cols], w_lo[:, layer, kb, cols])
                              for kb in range(KB)]).then_inc(unit_ready, 1)

                pe.wait_ge(bank_freed, value(UNITS, it, s, FREED0 + unit_t(KB - 1) + 1 - UNITS))
                for t in range(TILES):
                    lo, hi = t * P, (t + 1) * P
                    products(u_ps[t][:, lo:n_rows],
                             [(a_t[0][:, kb, lo:hi], a_t[1][:, kb, lo:hi],
                               a_t[0][:, kb, lo:n_rows], a_t[1][:, kb, lo:n_rows])
                              for kb in range(KB)]).then_inc(u_raw, 1)
                if s == 0:
                    pe.wait_ge(w_lo0_done, KB)
                if s == 2:
                    pe.wait_ge(w_lo1_done, KB)
                project(0, 0)
                project(0, 1)
                for t in range(1, TILES):
                    pe.wait_ge(off_copied, value(3, it, s, min(t + 1, 3)))
                    for above in range(t):
                        at = off_at[above] + (t - above - 1) * P
                        done = pe.transpose(u_ps[t][:, above * P:(above + 1) * P],
                                            u_off[:, at:at + P], ident[:, :])
                    done.then_inc(u_full, 1)
                for t in range(TILES):
                    for n in range(3):
                        if (t, n) not in ((0, 0), (0, 1)):
                            project(t, n)
                if t_units:
                    pe.wait_ge(h_done, value(TILES, it, s, 2 * TILES))
                    for db in range(KB):
                        pe.wait_ge(bank_freed, freed(it, s, unit_t(db) - ROT))
                        transpose_h(s, db)
                for kind, i in C_ORDER:
                    if kind == "E":
                        pe.wait_ge(masked, value(TILES, it, s, i + 1))
                        pe.wait_ge(bank_freed, freed(it, s, unit_e(i, t_units) - ROT))
                        for j in range(TILES):
                            done = pe.transpose(bank(s, unit_e(i, t_units))[:, j * P:(j + 1) * P],
                                                e_sb[:, i, j * P:(j + 1) * P], ident[:, :])
                        done.then_inc(unit_ready, 1)
                        continue
                    if i == 0:
                        pe.wait_ge(hw_lo_done, value(TILES, it, s, TILES))
                    pe.wait_ge(bank_freed, freed(it, s, unit_e(i, t_units)))
                    dst = bank(s, unit_c(i, t_units))[:, 0:dim]
                    off_diagonal = [(et_hi[:, i % 2, j * P:(j + 1) * P], et_lo[:, i % 2, j * P:(j + 1) * P],
                                     hw_hi[:, j, (j < i) * dim:((j < i) + 1) * dim],
                                     hw_lo[:, j, (j < i) * dim:((j < i) + 1) * dim])
                                    for j in range(TILES) if j != i]
                    products(dst, off_diagonal, last=False)
                    pe.wait_ge(dg_done, value(2 * TILES, it, s, 2 * (i + 1)))
                    diagonal = [(dg[:, i % 2, 0, n, :], dg[:, i % 2, 1, n, :],
                                 hw_hi[:, i, n * dim:(n + 1) * dim], hw_lo[:, i, n * dim:(n + 1) * dim])
                                for n in range(2)]
                    products(dst, diagonal, first=False).then_inc(unit_ready, 1)

            all_pairs(pe, lambda it, last: [step(it, s, last) for s in range(STEPS)])

        @block.scalar
        def _(act):
            def x_norm(count, g):
                act.wait_ge(x_chain, count * 3)
                for t in range(TILES):
                    act.activation(h[:, t, :], x_sb[g][:, t, :], ACT.Relu, bias=x_shift[:, t:t + 1],
                                   scale=x_rstd[:, t:t + 1]).then_inc(h_done, 1)

            def split_ht(parity, banks):
                for db, (src, count, _) in enumerate(banks):
                    act.wait_ge(unit_ready, count)
                    act.activation(ht_hi[:, parity, db, :], src, ACT.Copy).then_inc(ht_hi_done, 1)

            x_norm(1, 0)
            split_ht(0, [(rot_ps[(db - KB) % ROT][:, :], db + 1, None) for db in range(KB)])
            for c, (layer, kb) in enumerate(chunks):
                act.wait_ge(w_loaded[c % 2], 48 * (c // 2 + 1))
                act.activation(w_hi[:, layer, kb, :], w_stages[c % 2], ACT.Copy).then_inc(w_hi_done, 1)

            def step(it, s, last):
                t_units = 0 if last and s == STEPS - 1 else KB
                layer = s // 2

                def copy_off(t):
                    act.wait_ge(u_raw, value(TILES, it, s, t + 1))
                    width = (TILES - 1 - t) * P
                    act.activation(u_off[:, off_at[t]:off_at[t] + width], u_ps[t][:, (t + 1) * P:n_rows],
                                   ACT.Copy).then_inc(off_copied, 1)

                def exp(t):
                    act.wait_ge(max_done, value(TILES, it, s, t + 1))
                    act.activation(e_sb[:, t, :], u_ps[t][:, :], ACT.Exp, bias=neg_max[:, t:t + 1],
                                   scale=scale, accum_out=z_sum[:, t:t + 1]).then_inc(exp_done, 1)

                copy_off(0)
                copy_off(1)
                exp(0)
                copy_off(2)
                for t in range(1, TILES):
                    exp(t)
                for t in range(TILES):
                    act.wait_ge(bank_freed, freed(it, s, unit_p(t, 1)))
                    act.activation(hw_hi[:, t, :], proj[:, t % 2, :], ACT.Copy).then_inc(hw_hi_done, 1)
                if s in (1, 2):
                    for t in range(TILES):
                        act.wait_ge(affine_done, value(TILES, it, s, t + 1 - TILES))
                        act.activation(h[:, t, :], z[:, t, :], ACT.Relu).then_inc(h_done, 1)
                elif s == 0:
                    x_norm(it * 2 + 2, 1)
                elif not last:
                    x_norm(it * 2 + 3, 0)
                if t_units:
                    split_ht(1 - s % 2, [(bank(s, unit_t(db))[:, :], ready(it, s, unit_t(db)), None)
                                         for db in range(KB)])
                for i in range(TILES):
                    act.wait_ge(unit_ready, ready(it, s, unit_e(i, t_units)))
                    act.activation(et_hi[:, i % 2, :], bank(s, unit_e(i, t_units))[:, :], ACT.Copy).then_inc(et_hi_done, 1)
                if s in (0, 3):
                    act.wait_ge(out_stored, it * 32 + 16 * (1 + (s == 3)))
                else:
                    act.wait_ge(h_done, value(TILES, it, s, 2 * TILES))
                act.wait_ge(coef_chain, value(4, it, s, 4))
                for t in range(TILES):
                    act.activation(z[:, t, :], hs[:, t, :], ACT.Identity, bias=ln_shift[:, t:t + 1],
                                   scale=ln_scale[:, t:t + 1]).then_inc(z_done, 1)

            all_pairs(act, lambda it, last: [step(it, s, last) for s in range(STEPS)])

        @block.vector
        def _(dve):
            def x_statistics(g):
                for t in range(TILES):
                    dve.bn_stats(x_stats[:, t, :], x_sb[g][:, t, :]).then_inc(x_stats_done, 1)

            def x_variance(count):
                for t in range(TILES):
                    dve.bn_aggr(x_mv[:, t, :], x_stats[:, t, :]).then_inc(x_stats_done, 1)
                dve.wait_ge(x_stats_done, (count - 1) * XS + 2 * TILES)
                dve.tensor_scalar(x_var_eps[:, :], x_mv[:, :, 1], 1e-5, None, ALU.add).then_inc(x_stats_done, 1)

            def low_part(dst, src, hi):
                dve.tensor_tensor(dst, src, hi.bitcast(F32), ALU.subtract).then_inc(bank_freed, 1)

            def split_ht(parity, banks):
                for db, (src, count) in enumerate(banks):
                    dve.wait_ge(ht_hi_done, count)
                    low_part(ht_lo[:, parity, db, :], src, ht_hi[:, parity, db, :])

            dve.memset(diag_junk[:, :, :], 0.0).then_inc(bank_freed, CREDIT)
            dve.wait_ge(x_loaded[0], 16)
            x_statistics(0)
            dve.wait_ge(x_stats_done, TILES)
            x_variance(1)
            split_ht(0, [(rot_ps[(db - KB) % ROT][:, :], db + 1) for db in range(KB)])
            for c in range(KB):
                dve.wait_ge(w_hi_done, c + 1)
                dve.tensor_tensor(w_lo[:, 0, c, :], w_stages[c % 2], w_hi[:, 0, c, :].bitcast(F32),
                                  ALU.subtract).then_inc(w_lo0_done, 1)
            dve.wait_ge(consts, 6)
            dve.wait_ge(vec_loaded, 5 * 16)
            dve.wait_ge(bank_freed, CREDIT)

            def step(it, s, last):
                t_units = 0 if last and s == STEPS - 1 else KB
                g, layer = s % 2, s // 2

                def row_max(t):
                    if t == 0:
                        dve.wait_ge(off_copied, value(3, it, s, 1))
                    else:
                        dve.wait_ge(u_full, value(3, it, s, t))
                    dve.tensor_scalar(e_sb[:, t, :], u_ps[t][:, :], -scale, None, ALU.mult, ALU.min,
                                      accum_out=neg_max[:, t:t + 1]).then_inc(max_done, 1)

                def mask(t):
                    if t == 0:
                        dve.wait_ge(adj_loaded[g], it * 16 + 16)
                    dve.wait_ge(exp_done, value(TILES, it, s, t + 1))
                    dve.scalar_tensor_tensor(out=e_sb[:, t, :], in0=e_sb[:, t, :], scalar=1.0,
                                             in1=adj_sb[g][:, t, :], op0=ALU.mult, op1=ALU.mult,
                                             accum_out=e_sum[:, t:t + 1]).then_inc(masked, 1)

                def project(t, n):
                    dve.wait_ge(unit_ready, ready(it, s, unit_p(t, n)))
                    if n == 2:
                        dst = hs[:, t, :]
                    else:
                        if n == 0 and t >= 2:
                            dve.wait_ge(hw_lo_done, value(TILES, it, s, t - 1))
                        dst = proj[:, t % 2, n * dim:(n + 1) * dim]
                    dve.tensor_tensor(dst, bank(s, unit_p(t, n))[:, 0:dim], bias[:, layer, n, :],
                                      ALU.add).then_inc(bank_freed, 1)

                def diagonal(t):
                    dve.wait_ge(masked, value(TILES, it, s, t + 1))
                    dve.scalar_tensor_tensor(out=diag_junk[:, t, :], in0=e_sb[:, t, t * P:(t + 1) * P],
                                             scalar=1.0, in1=ident[:, :], op0=ALU.mult, op1=ALU.mult,
                                             accum_out=e_diag[:, t:t + 1]).then_inc(diag_done, 1)

                row_max(0)
                mask(0)
                project(0, 0)
                project(0, 1)
                for t in range(1, TILES):
                    row_max(t)
                project(0, 2)
                mask(1)
                project(1, 0)
                mask(2)
                project(1, 1)
                mask(3)
                project(1, 2)
                for t in range(TILES):
                    diagonal(t)
                for n in range(3):
                    project(2, n)
                dve.wait_ge(masked, value(TILES, it, s, TILES))
                dve.scalar_tensor_tensor(out=den[:, :], in0=z_sum[:, :], scalar=1e-10, in1=e_sum[:, :],
                                         op0=ALU.mult, op1=ALU.add).then_inc(recip_done, 1)
                dve.wait_ge(recip_done, value(4, it, s, 1))
                dve.reciprocal(recip[:, :], den[:, :]).then_inc(recip_done, 1)
                dve.wait_ge(recip_done, value(4, it, s, 2))
                dve.tensor_tensor(recip_sq[:, :], recip[:, :], recip[:, :], ALU.mult).then_inc(recip_done, 1)
                count, x_from = {0: (it * 2 + 2, 1), 3: (it * 2 + 3, 0)}.get(s, (None, None))
                if s == 3 and last:
                    count = None
                if count is not None:
                    dve.wait_ge(x_loaded[x_from], it * 16 + (16 if s == 0 else 32))
                    x_statistics(x_from)
                project(3, 0)
                if count is not None:
                    dve.wait_ge(x_stats_done, (count - 1) * XS + TILES)
                project(3, 1)
                if count is not None:
                    x_variance(count)
                project(3, 2)
                if t_units:
                    split_ht(1 - s % 2, [(bank(s, unit_t(db))[:, :], value(KB, it, s, KB + db + 1))
                                         for db in range(KB)])
                for kind, i in C_ORDER:
                    if kind == "E":
                        dve.wait_ge(et_hi_done, value(TILES, it, s, i + 1))
                        low_part(et_lo[:, i % 2, :], bank(s, unit_e(i, t_units))[:, :], et_hi[:, i % 2, :])
                        continue
                    if i == 0:
                        dve.wait_ge(diag_done, value(TILES, it, s, TILES))
                    dve.wait_ge(unit_ready, ready(it, s, unit_c(i, t_units)))
                    dve.scalar_tensor_tensor(out=hs[:, i, :], in0=hs[:, i, :], scalar=e_diag[:, i:i + 1],
                                             in1=bank(s, unit_c(i, t_units))[:, 0:dim], op0=ALU.mult,
                                             op1=ALU.add).then_inc(bank_freed, 1)
                    dve.wait_ge(bank_freed, freed(it, s, unit_c(i, t_units)))
                    dve.bn_stats(stats[:, i, :], hs[:, i, :]).then_inc(stats_done, 1)
                dve.wait_ge(stats_done, value(TILES, it, s, TILES))
                dve.tensor_scalar(neg_recip[:, :], recip[:, :], -1.0, None, ALU.mult).then_inc(recip_done, 1)
                for i in range(TILES):
                    dve.bn_aggr(mv[:, i, :], stats[:, i, :]).then_inc(aggr_done, 1)
                dve.wait_ge(recip_done, value(4, it, s, 4))
                for i in range(TILES):
                    dve.wait_ge(aggr_done, value(TILES, it, s, i + 1))
                    dve.tensor_scalar(var_eps[:, i:i + 1], mv[:, i, 1:2], recip_sq[:, i:i + 1], 1e-12,
                                      ALU.mult, ALU.add).then_inc(var_done, 1)
                if layer == 1:
                    for t in range(TILES):
                        dve.wait_ge(affine_done, value(TILES, it, s, t + 1))
                        dve.scalar_tensor_tensor(out=z[:, t, :], in0=z[:, t, :], scalar=0.0,
                                                 in1=x_sb[g][:, t, :], op0=ALU.max,
                                                 op1=ALU.add).then_inc(final_done, 1)

            all_pairs(dve, lambda it, last: [step(it, s, last) for s in range(STEPS)])

        @block.gpsimd
        def _(pool):
            pool.memset(ident[:, :], 0.0).then_inc(consts, 1)
            pool.memset(tri[:, :, :], 1.0).then_inc(consts, 1)
            pool.memset(minus_half[:, :], -0.5).then_inc(consts, 1)
            pool.wait_ge(consts, 3)
            pool.affine_select(out=ident[:, :], in_=ident[:, :], compare_op=ALU.not_equal, fill=1.0,
                               base=0, pattern=[[-1, P]], channel_multiplier=1).then_inc(consts, 1)
            pool.affine_select(out=tri[:, 0, :], in_=tri[:, 0, :], compare_op=ALU.is_gt, fill=0.0,
                               base=0, pattern=[[-1, P]], channel_multiplier=1).then_inc(consts, 1)
            pool.affine_select(out=tri[:, 1, :], in_=tri[:, 1, :], compare_op=ALU.is_gt, fill=0.0,
                               base=0, pattern=[[1, P]], channel_multiplier=-1).then_inc(consts, 1)
            pool.memset(minus_one[:, :], -1.0).then_inc(consts, 1)
            pool.memset(neg_recip[:, :], 0.0).then_inc(out_stored, 16)
            pool.wait_ge(consts, 7)

            def x_coefficients(count):
                base = (count - 1) * 3
                pool.wait_ge(x_stats_done, count * XS)
                pool.tensor_tensor(x_rstd[:, :], x_var_eps[:, :], minus_half[:, :], ALU.pow).then_inc(x_chain, 1)
                pool.wait_ge(x_chain, base + 1)
                pool.tensor_tensor(x_neg_rstd[:, :], x_rstd[:, :], minus_one[:, :], ALU.mult).then_inc(x_chain, 1)
                pool.wait_ge(x_chain, base + 2)
                pool.tensor_tensor(x_shift[:, :], x_neg_rstd[:, :], x_mv[:, :, 0], ALU.mult).then_inc(x_chain, 1)

            x_coefficients(1)
            for c in range(KB, 2 * KB):
                pool.wait_ge(w_hi_done, c + 1)
                pool.tensor_tensor(w_lo[:, 1, c - KB, :], w_stages[c % 2],
                                   w_hi[:, 1, c - KB, :].bitcast(F32), ALU.subtract).then_inc(w_lo1_done, 1)
            pool.wait_ge(vec_loaded, 5 * 16)

            def step(it, s, last):
                t_units = 0 if last and s == STEPS - 1 else KB
                layer = s // 2
                for t in range(TILES):
                    pool.wait_ge(hw_hi_done, value(TILES, it, s, t + 1))
                    pool.tensor_tensor(hw_lo[:, t, :], proj[:, t % 2, :], hw_hi[:, t, :].bitcast(F32),
                                       ALU.subtract).then_inc(hw_lo_done, 1)
                if s == 0:
                    x_coefficients(it * 2 + 2)
                elif s == 3 and not last:
                    x_coefficients(it * 2 + 3)
                for i in range(TILES):
                    for part, src in enumerate((et_hi, et_lo)):
                        if part == 0:
                            pool.wait_ge(et_hi_done, value(TILES, it, s, i + 1))
                        else:
                            pool.wait_ge(bank_freed, freed(it, s, unit_e(i, t_units)))
                        block_t = src[:, i % 2, i * P:(i + 1) * P].bitcast(F32)
                        pool.tensor_tensor(dg[:, i % 2, part, :, :], block_t.unsqueeze(1).to_broadcast([P, 2, P]),
                                           tri[:, :, :], ALU.mult).then_inc(dg_done, 1)
                pool.wait_ge(var_done, value(TILES, it, s, TILES))
                pool.tensor_tensor(rstd[:, :], var_eps[:, :], minus_half[:, :], ALU.pow).then_inc(coef_chain, 1)
                pool.wait_ge(coef_chain, value(4, it, s, 1))
                pool.tensor_tensor(neg_scale[:, :], rstd[:, :], neg_recip[:, :], ALU.mult).then_inc(coef_chain, 1)
                pool.tensor_tensor(ln_scale[:, :], rstd[:, :], recip[:, :], ALU.mult).then_inc(coef_chain, 1)
                pool.wait_ge(coef_chain, value(4, it, s, 2))
                pool.tensor_tensor(ln_shift[:, :], neg_scale[:, :], mv[:, :, 0], ALU.mult).then_inc(coef_chain, 1)
                for t in range(TILES):
                    pool.wait_ge(z_done, value(TILES, it, s, t + 1))
                    pool.tensor_tensor(z[:, t, :], z[:, t, :], gamma[:, layer, :], ALU.mult).then_inc(gamma_done, 1)
                    pool.wait_ge(gamma_done, value(TILES, it, s, t + 1))
                    pool.tensor_tensor(z[:, t, :], z[:, t, :], beta[:, layer, :], ALU.add).then_inc(affine_done, 1)

            all_pairs(pool, lambda it, last: [step(it, s, last) for s in range(STEPS)])


def kernel(x, adj, L0_gnn_Wl, L0_gnn_bl, L0_gnn_Ws, L0_gnn_bs, L0_gnn_Wr, L0_gnn_br, L0_gnn_ln_w, L0_gnn_ln_b):
    import numpy as np
    import concourse.bacc as bacc
    from concourse.bass_utils import run_bass_kernel_spmd

    nc = bacc.Bacc("TRN2", target_bir_lowering=False, num_devices=1)
    data = {
        "x": x, "adj": adj,
        "wl_t": np.transpose(L0_gnn_Wl, (0, 2, 1)), "bl": L0_gnn_bl,
        "ws_t": np.transpose(L0_gnn_Ws, (0, 2, 1)), "bs": L0_gnn_bs,
        "wr_t": np.transpose(L0_gnn_Wr, (0, 2, 1)), "br": L0_gnn_br,
        "ln_w": L0_gnn_ln_w, "ln_b": L0_gnn_ln_b,
    }
    arrays, args = {}, {}
    for name, value in data.items():
        a = np.ascontiguousarray(value)
        arrays[f"{name}_dram"] = a
        args[name] = nc.dram_tensor(f"{name}_dram", a.shape, mybir.dt.from_np(a.dtype), kind="ExternalInput").ap()
    args["out"] = nc.dram_tensor("out_dram", x.shape, F32, kind="ExternalOutput").ap()
    build_digcn(nc, **args)
    result = run_bass_kernel_spmd(nc, [arrays], core_ids=[0])
    return result.results[0]["out_dram"]
```

```python
from contextlib import ExitStack

import concourse.bass as bass
from concourse import mybir

F32 = mybir.dt.float32
F32R = mybir.dt.float32r
ALU = mybir.AluOpType
ACT = mybir.ActivationFunctionType

P = 128


def build_digcn(nc, x, adj, wl_t, bl, ws_t, bs, wr_t, br, ln_w, ln_b, out):
    n_graphs, n_rows, dim = x.shape
    layers = wl_t.shape[0]
    pairs = n_graphs // 2
    TILES = n_rows // P
    KB = dim // P
    scale = 1.0 / float(dim) ** 0.5
    STEPS = 2 * layers
    assert (TILES, layers) == (4, 2)

    ORDER = ([("P", t, n) for t in range(TILES) for n in range(3)][:-1]
             + [("E", 0), ("P", TILES - 1, 2), ("E", 1)] + [("T", db) for db in range(KB)]
             + [("C", 0), ("E", 2), ("C", 1), ("E", 3), ("C", 2), ("C", 3)])
    ORDER_LAST = [u for u in ORDER if u[0] != "T"]
    UNITS = len(ORDER)
    ROT = 4
    assert (UNITS * STEPS) % ROT == 0
    CREDIT = 8
    FREED0 = CREDIT + KB

    U_FROM = [0, 1, 2, 2]
    off_at = [0, 3 * P]

    ctx = ExitStack()
    with ctx:
        def sb(name, shape, dt=F32):
            return ctx.enter_context(nc.sbuf_tensor(name, shape, dt))

        def sem(name):
            return ctx.enter_context(nc.semaphore(name))

        ident = sb("ident", [P, P])
        tri = sb("tri", [P, 2, P])
        minus_half = sb("minus_half", [P, TILES])
        w_hi = sb("w_hi", [P, layers, KB, 3 * dim], F32R)
        w_lo = sb("w_lo", [P, layers, KB, 3 * dim], F32R)
        w_stage = sb("w_stage", [P, 3 * dim])
        bias = sb("bias", [P, layers, 3, dim])
        gamma = sb("gamma", [P, layers, dim])
        beta = sb("beta", [P, layers, dim])
        x_sb = [sb(f"x_{g}", [P, TILES, dim]) for g in "ab"]
        adj_sb = [sb(f"adj_{g}", [P, TILES, n_rows]) for g in "ab"]
        x_norm = sb("x_norm", [P, TILES, dim])
        ht_hi = sb("ht_hi", [P, 2, KB, n_rows], F32R)
        ht_lo = sb("ht_lo", [P, 2, KB, n_rows], F32R)
        u_off = sb("u_off", [P, 5 * P])
        e_sb = sb("e_sb", [P, TILES, n_rows])
        proj = sb("proj", [P, 2, 2 * dim])
        hw_hi = sb("hw_hi", [P, TILES, 2 * dim], F32R)
        hw_lo = sb("hw_lo", [P, TILES, 2 * dim], F32R)
        hs = sb("hs", [P, TILES, dim])
        et_hi = sb("et_hi", [P, 2, n_rows], F32R)
        et_lo = sb("et_lo", [P, 2, n_rows], F32R)
        dg = sb("dg", [P, 2, 2, 2, P], F32R)
        z = sb("z", [P, TILES, dim])
        diag_junk = sb("diag_junk", [P, TILES, P])
        neg_max = sb("neg_max", [P, TILES])
        z_sum = sb("z_sum", [P, TILES])
        e_sum = sb("e_sum", [P, TILES])
        e_diag = sb("e_diag", [P, TILES])
        den = sb("den", [P, TILES])
        recip = sb("recip", [P, TILES])
        recip_sq = sb("recip_sq", [P, TILES])
        stats = sb("stats", [P, TILES, 6])
        mv = sb("mv", [P, TILES, 2])
        var_eps = sb("var_eps", [P, TILES])
        rstd = sb("rstd", [P, TILES])
        ln_scale = sb("ln_scale", [P, TILES])
        x_stats = sb("x_stats", [P, TILES, 6])
        x_mv = sb("x_mv", [P, TILES, 2])
        x_var_eps = sb("x_var_eps", [P, TILES])
        x_rstd = sb("x_rstd", [P, TILES])
        x_shift = sb("x_shift", [P, TILES])

        u_ps = [ctx.enter_context(nc.psum_tensor(f"u_ps{t}", [P, n_rows], F32)) for t in range(TILES)]
        rot_ps = [ctx.enter_context(nc.psum_tensor(f"rot_ps{t}", [P, n_rows], F32)) for t in range(ROT)]

        u_raw = sem("u_raw")
        u_full = sem("u_full")
        unit_ready = sem("unit_ready")
        off_copied = sem("off_copied")
        exp_done = sem("exp_done")
        hw_hi_done = sem("hw_hi_done")
        hw_lo_done = sem("hw_lo_done")
        x_shift_done = sem("x_shift_done")
        x_norm_done = sem("x_norm_done")
        ht_hi_done = sem("ht_hi_done")
        et_hi_done = sem("et_hi_done")
        max_done = sem("max_done")
        masked = sem("masked")
        diag_done = sem("diag_done")
        recip_done = sem("recip_done")
        bank_freed = sem("bank_freed")
        stats_done = sem("stats_done")
        aggr_done = sem("aggr_done")
        var_done = sem("var_done")
        final_done = sem("final_done")
        dg_done = sem("dg_done")
        centred = sem("centred")
        scale_done = sem("scale_done")
        affine_done = sem("affine_done")
        rstd_done = sem("rstd_done")
        x_rstd_done = sem("x_rstd_done")
        x_stats_done = sem("x_stats_done")
        x_loaded = [sem(f"x_loaded_{g}") for g in "ab"]
        x_first = [sem(f"x_first_{t}") for t in range(TILES)]
        adj_loaded = [sem(f"adj_loaded_{g}") for g in "ab"]
        out_stored = sem("out_stored")
        consts = sem("consts")
        vec_loaded = sem("vec_loaded")
        w_loaded = [sem("w_loaded_even"), sem("w_loaded_odd")]
        w_hi_done = sem("w_hi_done")
        w_lo0_done = sem("w_lo0_done")
        w_lo1_done = sem("w_lo1_done")

        XS = 2 * TILES + 1

        def bank(s, unit):
            return rot_ps[(UNITS * s + unit) % ROT]

        def value(per_step, it, s, count):
            return it * (STEPS * per_step) + (per_step * s + count)

        def ready(it, s, unit):
            return value(UNITS, it, s, KB + unit + 1)

        def freed(it, s, unit):
            return value(UNITS, it, s, FREED0 + unit + 1)

        def all_pairs(eng, body):
            if pairs > 1:
                with eng.Fori(0, pairs - 1) as it:
                    body(it, False)
            body(pairs - 1, True)

        def rows(dram, graph):
            return dram[graph].rearrange("(t p) n -> p t n", p=P)

        w_parts = [wl_t, wr_t, ws_t]
        chunks = [(layer, kb) for layer in range(layers) for kb in range(KB)]
        z_flat = z[:, :, :].rearrange("p t n -> p (t n)")
        w_stages = [w_stage[:, :], z_flat[:, 0:3 * dim]]

        block = ctx.enter_context(nc.Block())

        @block.sync
        def _(sp):
            def load_w(c):
                layer, kb = chunks[c]
                for n, part in enumerate(w_parts):
                    sp.dma_start(w_stages[c % 2][:, n * dim:(n + 1) * dim],
                                 part[layer, kb * P:(kb + 1) * P, :]).then_inc(w_loaded[c % 2], 16)

            for t in range(TILES):
                sp.dma_start(x_sb[0][:, t, :], rows(x, 0)[:, t, :]).then_inc(x_first[t], 16)
            load_w(0)
            load_w(1)
            sp.dma_start(adj_sb[0][:, :, :], rows(adj, 0)).then_inc(adj_loaded[0], 16)
            for tile, vec in ((bias[:, :, 0, :], bl), (bias[:, :, 1, :], br), (bias[:, :, 2, :], bs),
                              (gamma[:, :, :], ln_w), (beta[:, :, :], ln_b)):
                sp.dma_start(tile, vec.partition_broadcast(P)).then_inc(vec_loaded, 16)
            sp.dma_start(x_sb[1][:, :, :], rows(x, 1)).then_inc(x_loaded[1], 16)
            for c in range(2, len(chunks)):
                if c - 2 < KB:
                    sp.wait_ge(w_lo0_done, c - 1)
                else:
                    sp.wait_ge(w_lo1_done, c - 1 - KB)
                load_w(c)
            sp.dma_start(adj_sb[1][:, :, :], rows(adj, 1)).then_inc(adj_loaded[1], 16)

            def pair(it, last):
                for g in range(2):
                    s = 2 + g
                    if not last:
                        sp.wait_ge(masked, value(TILES, it, s, TILES))
                        sp.dma_start(adj_sb[g][:, :, :], rows(adj, it * 2 + (2 + g))).then_inc(adj_loaded[g], 16)
                    for t in range(TILES):
                        sp.wait_ge(final_done, it * (2 * TILES) + (TILES * g + t + 1))
                        sp.dma_start(rows(out, it * 2 + g)[:, t, :], z[:, t, :]).then_inc(out_stored, 16)
                    if not last:
                        sp.dma_start(x_sb[g][:, :, :], rows(x, it * 2 + (2 + g))).then_inc(x_loaded[g], 16)

            all_pairs(sp, pair)
            sp.wait_ge(out_stored, 16 * (n_graphs * TILES + 1))

        @block.tensor
        def _(pe):
            def products(dst, pairs_of_operands, first=True, last=True):
                n = len(pairs_of_operands)
                for m, (a_hi, a_lo, b_hi, b_lo) in enumerate(pairs_of_operands):
                    pe.matmul(dst, a_hi, b_hi, start=first and m == 0, stop=False)
                    pe.matmul(dst, a_hi, b_lo, start=False, stop=False)
                    done = pe.matmul(dst, a_lo, b_hi, start=False, stop=last and m == n - 1)
                return done

            pe.wait_ge(consts, 6)
            pe.wait_ge(x_norm_done, TILES)
            for db in range(KB):
                for t in range(TILES):
                    done = pe.transpose(rot_ps[(db - KB) % ROT][:, t * P:(t + 1) * P],
                                        x_norm[:, t, db * P:(db + 1) * P], ident[:, :])
                done.then_inc(unit_ready, 1)
            pe.wait_ge(bank_freed, FREED0)

            def step(it, s, last):
                order = ORDER_LAST if last and s == STEPS - 1 else ORDER

                def unit(*what):
                    return order.index(what)

                cur, layer = s % 2, s // 2
                a_t = [ht_hi[:, cur], ht_lo[:, cur]]

                def project(t, n):
                    pe.wait_ge(bank_freed, freed(it, s, unit("P", t, n) - ROT))
                    lo, hi = t * P, (t + 1) * P
                    cols = slice(n * dim, (n + 1) * dim)
                    products(bank(s, unit("P", t, n))[:, 0:dim],
                             [(a_t[0][:, kb, lo:hi], a_t[1][:, kb, lo:hi],
                               w_hi[:, layer, kb, cols], w_lo[:, layer, kb, cols])
                              for kb in range(KB)]).then_inc(unit_ready, 1)

                def transpose_h(db):
                    src = z if s in (1, 2) else x_norm
                    pe.wait_ge(bank_freed, freed(it, s, unit("T", db) - ROT))
                    for t in range(TILES):
                        done = pe.transpose(bank(s, unit("T", db))[:, t * P:(t + 1) * P],
                                            src[:, t, db * P:(db + 1) * P], ident[:, :])
                    done.then_inc(unit_ready, 1)

                def transpose_e(i):
                    pe.wait_ge(masked, value(TILES, it, s, i + 1))
                    pe.wait_ge(bank_freed, freed(it, s, unit("E", i) - ROT))
                    for j in range(TILES):
                        done = pe.transpose(bank(s, unit("E", i))[:, j * P:(j + 1) * P],
                                            e_sb[:, i, j * P:(j + 1) * P], ident[:, :])
                    done.then_inc(unit_ready, 1)

                def attend(i):
                    pe.wait_ge(bank_freed, freed(it, s, max(unit("E", i), unit("C", i) - ROT)))
                    dst = bank(s, unit("C", i))[:, 0:dim]
                    for m, j in enumerate(j for j in range(TILES) if j != i):
                        if i == 0:
                            pe.wait_ge(hw_lo_done, value(TILES, it, s, j + 1))
                        cols = slice((j < i) * dim, ((j < i) + 1) * dim)
                        products(dst, [(et_hi[:, i % 2, j * P:(j + 1) * P], et_lo[:, i % 2, j * P:(j + 1) * P],
                                        hw_hi[:, j, cols], hw_lo[:, j, cols])], first=m == 0, last=False)
                    pe.wait_ge(dg_done, value(2 * TILES, it, s, 2 * (i + 1)))
                    products(dst, [(dg[:, i % 2, 0, n, :], dg[:, i % 2, 1, n, :],
                                    hw_hi[:, i, n * dim:(n + 1) * dim], hw_lo[:, i, n * dim:(n + 1) * dim])
                                   for n in range(2)], first=False).then_inc(unit_ready, 1)

                pe.wait_ge(bank_freed, value(UNITS, it, s, FREED0 + ORDER.index(("T", KB - 1)) + 1 - UNITS))
                for t in range(TILES):
                    lo, hi = t * P, (t + 1) * P
                    left = U_FROM[t] * P
                    products(u_ps[t][:, left:n_rows],
                             [(a_t[0][:, kb, lo:hi], a_t[1][:, kb, lo:hi],
                               a_t[0][:, kb, left:n_rows], a_t[1][:, kb, left:n_rows])
                              for kb in range(KB)]).then_inc(u_raw, 1)
                if s == 0:
                    pe.wait_ge(w_lo0_done, KB)
                if s == 2:
                    pe.wait_ge(w_lo1_done, KB)
                project(0, 0)
                project(0, 1)
                for t in range(1, TILES):
                    if t < TILES - 1:
                        pe.wait_ge(off_copied, value(2, it, s, min(t + 1, 2)))
                    for above in range(U_FROM[t]):
                        at = off_at[above] + (t - above - 1) * P
                        done = pe.transpose(u_ps[t][:, above * P:(above + 1) * P],
                                            u_off[:, at:at + P], ident[:, :])
                    done.then_inc(u_full, 1)
                for what in order[2:]:
                    if what[0] == "P":
                        project(*what[1:])
                    elif what[0] == "T":
                        if what[1] == 0:
                            if s in (1, 2):
                                pe.wait_ge(affine_done, value(TILES, it, s, 0))
                            else:
                                pe.wait_ge(x_norm_done, value(2, it, 0, 8 if s == 0 else 12))
                        transpose_h(what[1])
                    elif what[0] == "E":
                        transpose_e(what[1])
                    else:
                        attend(what[1])

            all_pairs(pe, lambda it, last: [step(it, s, last) for s in range(STEPS)])

        @block.scalar
        def _(act):
            def x_normalise(count, g):
                act.wait_ge(x_shift_done, count)
                for t in range(TILES):
                    act.activation(x_norm[:, t, :], x_sb[g][:, t, :], ACT.Identity, bias=x_shift[:, t:t + 1],
                                   scale=x_rstd[:, t:t + 1]).then_inc(x_norm_done, 1)

            def split_ht(parity, banks):
                for db, (src, count, _) in enumerate(banks):
                    act.wait_ge(unit_ready, count)
                    act.activation(ht_hi[:, parity, db, :], src, ACT.Relu).then_inc(ht_hi_done, 1)

            x_normalise(1, 0)
            split_ht(0, [(rot_ps[(db - KB) % ROT][:, :], db + 1, None) for db in range(KB)])
            for c, (layer, kb) in enumerate(chunks):
                act.wait_ge(w_loaded[c % 2], 48 * (c // 2 + 1))
                act.activation(w_hi[:, layer, kb, :], w_stages[c % 2], ACT.Copy).then_inc(w_hi_done, 1)

            def step(it, s, last):
                order = ORDER_LAST if last and s == STEPS - 1 else ORDER

                def unit(*what):
                    return order.index(what)

                def copy_off(t):
                    act.wait_ge(u_raw, value(TILES, it, s, t + 1))
                    width = (TILES - 1 - t) * P
                    act.activation(u_off[:, off_at[t]:off_at[t] + width], u_ps[t][:, (t + 1) * P:n_rows],
                                   ACT.Copy).then_inc(off_copied, 1)

                def exp(t):
                    act.wait_ge(max_done, value(TILES, it, s, t + 1))
                    act.activation(e_sb[:, t, :], u_ps[t][:, :], ACT.Exp, bias=neg_max[:, t:t + 1],
                                   scale=scale, accum_out=z_sum[:, t:t + 1]).then_inc(exp_done, 1)

                for t in range(2):
                    copy_off(t)
                for t in range(TILES):
                    exp(t)

                def split_proj(t):
                    act.wait_ge(bank_freed, freed(it, s, unit("P", t, 1)))
                    act.activation(hw_hi[:, t, :], proj[:, t % 2, :], ACT.Copy).then_inc(hw_hi_done, 1)

                def split_e(i):
                    act.wait_ge(unit_ready, ready(it, s, unit("E", i)))
                    act.activation(et_hi[:, i % 2, :], bank(s, unit("E", i))[:, :], ACT.Copy).then_inc(et_hi_done, 1)

                for t in range(TILES - 1):
                    split_proj(t)
                if s == 0:
                    x_normalise(it * 2 + 2, 1)
                elif s == STEPS - 1 and not last:
                    x_normalise(it * 2 + 3, 0)
                split_proj(TILES - 1)
                split_e(0)
                split_e(1)
                if order is ORDER:
                    split_ht(1 - s % 2, [(bank(s, unit("T", db))[:, :], ready(it, s, unit("T", db)), None)
                                         for db in range(KB)])
                split_e(2)
                split_e(3)

            all_pairs(act, lambda it, last: [step(it, s, last) for s in range(STEPS)])

        @block.vector
        def _(dve):
            def x_statistics(g, first=False):
                for t in range(TILES):
                    if first:
                        dve.wait_ge(x_first[t], 16)
                    dve.bn_stats(x_stats[:, t, :], x_sb[g][:, t, :]).then_inc(x_stats_done, 1)

            def x_variance(count):
                for t in range(TILES):
                    dve.bn_aggr(x_mv[:, t, :], x_stats[:, t, :]).then_inc(x_stats_done, 1)
                dve.wait_ge(x_stats_done, (count - 1) * XS + 2 * TILES)
                dve.tensor_scalar(x_var_eps[:, :], x_mv[:, :, 1], 1e-5, None, ALU.add).then_inc(x_stats_done, 1)

            def x_shift_of(count):
                dve.wait_ge(x_rstd_done, count)
                dve.scalar_tensor_tensor(out=x_shift[:, :], in0=x_mv[:, :, 0], scalar=-1.0, in1=x_rstd[:, :],
                                         op0=ALU.mult, op1=ALU.mult).then_inc(x_shift_done, 1)

            def low_part(dst, src, hi):
                dve.tensor_tensor(dst, src, hi.bitcast(F32), ALU.subtract).then_inc(bank_freed, 1)

            def split_ht(parity, banks):
                for db, (src, count) in enumerate(banks):
                    dve.wait_ge(ht_hi_done, count)
                    dve.scalar_tensor_tensor(out=ht_lo[:, parity, db, :], in0=src, scalar=0.0,
                                             in1=ht_hi[:, parity, db, :].bitcast(F32), op0=ALU.max,
                                             op1=ALU.subtract).then_inc(bank_freed, 1)

            dve.memset(diag_junk[:, :, :], 0.0).then_inc(bank_freed, CREDIT)
            x_statistics(0, first=True)
            dve.wait_ge(x_stats_done, TILES)
            x_variance(1)
            x_shift_of(1)
            split_ht(0, [(rot_ps[(db - KB) % ROT][:, :], db + 1) for db in range(KB)])
            for c in range(KB):
                dve.wait_ge(w_hi_done, c + 1)
                dve.tensor_tensor(w_lo[:, 0, c, :], w_stages[c % 2], w_hi[:, 0, c, :].bitcast(F32),
                                  ALU.subtract).then_inc(w_lo0_done, 1)
            dve.wait_ge(consts, 6)
            dve.wait_ge(vec_loaded, 5 * 16)
            dve.wait_ge(bank_freed, CREDIT)

            def step(it, s, last):
                order = ORDER_LAST if last and s == STEPS - 1 else ORDER

                def unit(*what):
                    return order.index(what)

                g, layer = s % 2, s // 2

                def row_max(t):
                    if t == 0:
                        dve.wait_ge(off_copied, value(2, it, s, 1))
                    else:
                        dve.wait_ge(u_full, value(3, it, s, t))
                    dve.tensor_scalar(e_sb[:, t, :], u_ps[t][:, :], -scale, None, ALU.mult, ALU.min,
                                      accum_out=neg_max[:, t:t + 1]).then_inc(max_done, 1)

                def mask(t):
                    if t == 0:
                        dve.wait_ge(adj_loaded[g], it * 16 + 16)
                    dve.wait_ge(exp_done, value(TILES, it, s, t + 1))
                    dve.scalar_tensor_tensor(out=e_sb[:, t, :], in0=e_sb[:, t, :], scalar=1.0,
                                             in1=adj_sb[g][:, t, :], op0=ALU.mult, op1=ALU.mult,
                                             accum_out=e_sum[:, t:t + 1]).then_inc(masked, 1)

                def project(t, n):
                    dve.wait_ge(unit_ready, ready(it, s, unit("P", t, n)))
                    if n == 2:
                        dst = hs[:, t, :]
                    else:
                        if n == 0 and t >= 2:
                            dve.wait_ge(hw_lo_done, value(TILES, it, s, t - 1))
                        dst = proj[:, t % 2, n * dim:(n + 1) * dim]
                    dve.tensor_tensor(dst, bank(s, unit("P", t, n))[:, 0:dim], bias[:, layer, n, :],
                                      ALU.add).then_inc(bank_freed, 1)

                def diagonal(t):
                    dve.wait_ge(masked, value(TILES, it, s, t + 1))
                    dve.scalar_tensor_tensor(out=diag_junk[:, t, :], in0=e_sb[:, t, t * P:(t + 1) * P],
                                             scalar=1.0, in1=ident[:, :], op0=ALU.mult, op1=ALU.mult,
                                             accum_out=e_diag[:, t:t + 1]).then_inc(diag_done, 1)

                row_max(0)
                project(0, 0)
                project(0, 1)
                mask(0)
                for t in range(1, TILES):
                    row_max(t)
                project(0, 2)
                mask(1)
                project(1, 0)
                mask(2)
                project(1, 1)
                mask(3)
                project(1, 2)
                dve.wait_ge(masked, value(TILES, it, s, TILES))
                dve.scalar_tensor_tensor(out=den[:, :], in0=z_sum[:, :], scalar=1e-10, in1=e_sum[:, :],
                                         op0=ALU.mult, op1=ALU.add).then_inc(recip_done, 1)
                dve.wait_ge(recip_done, value(3, it, s, 1))
                dve.reciprocal(recip[:, :], den[:, :]).then_inc(recip_done, 1)
                dve.wait_ge(recip_done, value(3, it, s, 2))
                dve.tensor_tensor(recip_sq[:, :], recip[:, :], recip[:, :], ALU.mult).then_inc(recip_done, 1)
                count, x_from = {0: (it * 2 + 2, 1), 3: (it * 2 + 3, 0)}.get(s, (None, None))
                if order is not ORDER:
                    count = None
                if count is not None:
                    dve.wait_ge(x_loaded[x_from], it * 16 + 16)
                    x_statistics(x_from)
                project(2, 0)
                if count is not None:
                    dve.wait_ge(x_stats_done, (count - 1) * XS + TILES)
                project(2, 1)
                if count is not None:
                    x_variance(count)
                project(2, 2)
                if count is not None:
                    x_shift_of(count)

                def split_e(i):
                    dve.wait_ge(et_hi_done, value(TILES, it, s, i + 1))
                    low_part(et_lo[:, i % 2, :], bank(s, unit("E", i))[:, :], et_hi[:, i % 2, :])

                def variance(i):
                    dve.wait_ge(aggr_done, value(TILES, it, s, i + 1))
                    dve.tensor_scalar(var_eps[:, i:i + 1], mv[:, i, 1:2], recip_sq[:, i:i + 1], 1e-12,
                                      ALU.mult, ALU.add).then_inc(var_done, 1)

                def centre(i):
                    if i == 0 and s in (0, 3):
                        dve.wait_ge(out_stored, it * 128 + 16 * (1 + (s == 3) * TILES))
                    dve.scalar_tensor_tensor(out=z[:, i, :], in0=hs[:, i, :], scalar=mv[:, i, 0:1],
                                             in1=gamma[:, layer, :], op0=ALU.subtract,
                                             op1=ALU.mult).then_inc(centred, 1)

                def finish(i):
                    if i == 0:
                        for t in range(TILES):
                            diagonal(t)
                        dve.wait_ge(diag_done, value(TILES, it, s, TILES))
                    else:
                        dve.wait_ge(stats_done, value(TILES, it, s, i))
                    dve.wait_ge(unit_ready, ready(it, s, unit("C", i)))
                    dve.scalar_tensor_tensor(out=hs[:, i, :], in0=hs[:, i, :], scalar=e_diag[:, i:i + 1],
                                             in1=bank(s, unit("C", i))[:, 0:dim], op0=ALU.mult,
                                             op1=ALU.add).then_inc(bank_freed, 1)
                    if i > 0:
                        dve.bn_aggr(mv[:, i - 1, :], stats[:, i - 1, :]).then_inc(aggr_done, 1)
                    dve.wait_ge(bank_freed, freed(it, s, unit("C", i)))
                    dve.bn_stats(stats[:, i, :], hs[:, i, :]).then_inc(stats_done, 1)
                    if 0 < i < TILES - 1:
                        variance(i - 1)
                        centre(i - 1)

                for what in order[order.index(("P", 3, 0)):]:
                    if what[0] == "P":
                        project(*what[1:])
                    elif what == ("T", 0):
                        split_ht(1 - s % 2, [(bank(s, unit("T", db))[:, :], value(KB, it, s, KB + db + 1))
                                             for db in range(KB)])
                    elif what[0] == "E":
                        split_e(what[1])
                    elif what[0] == "C":
                        finish(what[1])
                dve.wait_ge(stats_done, value(TILES, it, s, TILES))
                variance(TILES - 2)
                dve.bn_aggr(mv[:, TILES - 1, :], stats[:, TILES - 1, :]).then_inc(aggr_done, 1)
                variance(TILES - 1)
                centre(TILES - 2)
                centre(TILES - 1)
                dve.wait_ge(rstd_done, value(1, it, s, 1))
                dve.tensor_tensor(ln_scale[:, :], rstd[:, :], recip[:, :], ALU.mult).then_inc(scale_done, 1)
                dve.wait_ge(scale_done, value(1, it, s, 1))
                for t in range(TILES):
                    dve.wait_ge(centred, value(TILES, it, s, t + 1))
                    dve.scalar_tensor_tensor(out=z[:, t, :], in0=z[:, t, :], scalar=ln_scale[:, t:t + 1],
                                             in1=beta[:, layer, :], op0=ALU.mult,
                                             op1=ALU.add).then_inc(affine_done, 1)
                if layer == 1:
                    for t in range(TILES):
                        dve.wait_ge(affine_done, value(TILES, it, s, t + 1))
                        dve.scalar_tensor_tensor(out=z[:, t, :], in0=z[:, t, :], scalar=0.0,
                                                 in1=x_sb[g][:, t, :], op0=ALU.max,
                                                 op1=ALU.add).then_inc(final_done, 1)

            all_pairs(dve, lambda it, last: [step(it, s, last) for s in range(STEPS)])

        @block.gpsimd
        def _(pool):
            pool.memset(ident[:, :], 0.0).then_inc(consts, 1)
            pool.memset(tri[:, :, :], 1.0).then_inc(consts, 1)
            pool.memset(minus_half[:, :], -0.5).then_inc(consts, 1)
            pool.wait_ge(consts, 3)
            pool.affine_select(out=ident[:, :], in_=ident[:, :], compare_op=ALU.not_equal, fill=1.0,
                               base=0, pattern=[[-1, P]], channel_multiplier=1).then_inc(consts, 1)
            pool.affine_select(out=tri[:, 0, :], in_=tri[:, 0, :], compare_op=ALU.is_gt, fill=0.0,
                               base=0, pattern=[[-1, P]], channel_multiplier=1).then_inc(consts, 1)
            pool.affine_select(out=tri[:, 1, :], in_=tri[:, 1, :], compare_op=ALU.is_gt, fill=0.0,
                               base=0, pattern=[[1, P]], channel_multiplier=-1).then_inc(consts, 1)
            pool.memset(rstd[:, :], 0.0).then_inc(out_stored, 16)

            def x_rstd_of(count):
                pool.wait_ge(x_stats_done, count * XS)
                pool.tensor_tensor(x_rstd[:, :], x_var_eps[:, :], minus_half[:, :], ALU.pow).then_inc(x_rstd_done, 1)

            x_rstd_of(1)
            for c in range(KB, 2 * KB):
                pool.wait_ge(w_hi_done, c + 1)
                pool.tensor_tensor(w_lo[:, 1, c - KB, :], w_stages[c % 2],
                                   w_hi[:, 1, c - KB, :].bitcast(F32), ALU.subtract).then_inc(w_lo1_done, 1)
            pool.wait_ge(vec_loaded, 5 * 16)

            def step(it, s, last):
                order = ORDER_LAST if last and s == STEPS - 1 else ORDER

                def unit(*what):
                    return order.index(what)

                for t in range(TILES):
                    if t == 2 and s == 0:
                        x_rstd_of(it * 2 + 2)
                    elif t == 2 and s == 3 and not last:
                        x_rstd_of(it * 2 + 3)
                    pool.wait_ge(hw_hi_done, value(TILES, it, s, t + 1))
                    pool.tensor_tensor(hw_lo[:, t, :], proj[:, t % 2, :], hw_hi[:, t, :].bitcast(F32),
                                       ALU.subtract).then_inc(hw_lo_done, 1)
                for i in range(TILES):
                    for part, src in enumerate((et_hi, et_lo)):
                        if part == 0:
                            pool.wait_ge(et_hi_done, value(TILES, it, s, i + 1))
                        else:
                            pool.wait_ge(bank_freed, freed(it, s, unit("E", i)))
                        block_t = src[:, i % 2, i * P:(i + 1) * P].bitcast(F32)
                        pool.tensor_tensor(dg[:, i % 2, part, :, :], block_t.unsqueeze(1).to_broadcast([P, 2, P]),
                                           tri[:, :, :], ALU.mult).then_inc(dg_done, 1)
                pool.wait_ge(var_done, value(TILES, it, s, TILES))
                pool.tensor_tensor(rstd[:, :], var_eps[:, :], minus_half[:, :], ALU.pow).then_inc(rstd_done, 1)

            all_pairs(pool, lambda it, last: [step(it, s, last) for s in range(STEPS)])


def kernel(x, adj, L0_gnn_Wl, L0_gnn_bl, L0_gnn_Ws, L0_gnn_bs, L0_gnn_Wr, L0_gnn_br, L0_gnn_ln_w, L0_gnn_ln_b):
    import numpy as np
    import concourse.bacc as bacc
    from concourse.bass_utils import run_bass_kernel_spmd

    nc = bacc.Bacc("TRN2", target_bir_lowering=False, num_devices=1)
    data = {
        "x": x, "adj": adj,
        "wl_t": np.transpose(L0_gnn_Wl, (0, 2, 1)), "bl": L0_gnn_bl,
        "ws_t": np.transpose(L0_gnn_Ws, (0, 2, 1)), "bs": L0_gnn_bs,
        "wr_t": np.transpose(L0_gnn_Wr, (0, 2, 1)), "br": L0_gnn_br,
        "ln_w": L0_gnn_ln_w, "ln_b": L0_gnn_ln_b,
    }
    arrays, args = {}, {}
    for name, value in data.items():
        a = np.ascontiguousarray(value)
        arrays[f"{name}_dram"] = a
        args[name] = nc.dram_tensor(f"{name}_dram", a.shape, mybir.dt.from_np(a.dtype), kind="ExternalInput").ap()
    args["out"] = nc.dram_tensor("out_dram", x.shape, F32, kind="ExternalOutput").ap()
    build_digcn(nc, **args)
    result = run_bass_kernel_spmd(nc, [arrays], core_ids=[0])
    return result.results[0]["out_dram"]
```

```python
from contextlib import ExitStack

import concourse.bass as bass
from concourse import mybir

F32 = mybir.dt.float32
F32R = mybir.dt.float32r
ALU = mybir.AluOpType
ACT = mybir.ActivationFunctionType

P = 128


def build_digcn(nc, x, adj, wl_t, bl, ws_t, bs, wr_t, br, ln_w, ln_b, out):
    n_graphs, n_rows, dim = x.shape
    layers = wl_t.shape[0]
    pairs = n_graphs // 2
    assert pairs > 2
    TILES = n_rows // P
    KB = dim // P
    scale = 1.0 / float(dim) ** 0.5
    STEPS = 2 * layers
    assert (TILES, layers) == (4, 2)

    ORDER = ([("P", t, n) for t in range(TILES) for n in range(3)][:-1]
             + [("E", 0), ("E", 1), ("P", TILES - 1, 2)] + [("T", db) for db in range(KB)]
             + [("C", 0), ("E", 2), ("C", 1), ("E", 3), ("C", 2), ("C", 3)])
    ORDER_LAST = [u for u in ORDER if u[0] != "T"]
    UNITS = len(ORDER)
    ROT = 4
    assert (UNITS * STEPS) % ROT == 0
    CREDIT = 8
    FREED0 = CREDIT + KB

    U_FROM = [0, 1, 2, 2]
    off_at = [0, 3 * P]

    ctx = ExitStack()
    with ctx:
        def sb(name, shape, dt=F32):
            return ctx.enter_context(nc.sbuf_tensor(name, shape, dt))

        def sem(name):
            return ctx.enter_context(nc.semaphore(name))

        ident = sb("ident", [P, P])
        tri = sb("tri", [P, 2, P])
        minus_half = sb("minus_half", [P, TILES])
        w_hi = sb("w_hi", [P, layers, KB, 3 * dim], F32R)
        w_lo = sb("w_lo", [P, layers, KB, 3 * dim], F32R)
        w_stage = sb("w_stage", [P, 2, 3 * dim])
        bias = sb("bias", [P, layers, 3, dim])
        gamma = sb("gamma", [P, layers, dim])
        beta = sb("beta", [P, layers, dim])
        x_sb = [sb(f"x_{g}", [P, TILES, dim]) for g in "ab"]
        adj_sb = [sb(f"adj_{g}", [P, TILES, n_rows]) for g in "ab"]
        x_norm = sb("x_norm", [P, TILES, dim])
        ht_hi = sb("ht_hi", [P, 2, KB, n_rows], F32R)
        ht_lo = sb("ht_lo", [P, 2, KB, n_rows], F32R)
        u_off = sb("u_off", [P, 5 * P])
        e_sb = sb("e_sb", [P, TILES, n_rows])
        proj = sb("proj", [P, 2, 2 * dim])
        hw_hi = sb("hw_hi", [P, TILES, 2 * dim], F32R)
        hw_lo = sb("hw_lo", [P, TILES, 2 * dim], F32R)
        hs = sb("hs", [P, TILES, dim])
        et_hi = sb("et_hi", [P, 2, n_rows], F32R)
        et_lo = sb("et_lo", [P, 2, n_rows], F32R)
        dg = sb("dg", [P, 2, 2, 2, P], F32R)
        z = sb("z", [P, TILES, dim])
        diag_junk = sb("diag_junk", [P, TILES, P])
        neg_max = sb("neg_max", [P, TILES])
        z_sum = sb("z_sum", [P, TILES])
        e_sum = sb("e_sum", [P, TILES])
        e_diag = sb("e_diag", [P, TILES])
        den = sb("den", [P, TILES])
        recip = sb("recip", [P, TILES])
        recip_sq = sb("recip_sq", [P, TILES])
        stats = sb("stats", [P, TILES, 6])
        mv = sb("mv", [P, TILES, 2])
        var_eps = sb("var_eps", [P, TILES])
        rstd = sb("rstd", [P, TILES])
        ln_scale = sb("ln_scale", [P, TILES])
        x_stats = sb("x_stats", [P, TILES, 6])
        x_mv = sb("x_mv", [P, TILES, 2])
        x_var_eps = sb("x_var_eps", [P, TILES])
        x_rstd = sb("x_rstd", [P, TILES])
        x_shift = sb("x_shift", [P, TILES])

        u_ps = [ctx.enter_context(nc.psum_tensor(f"u_ps{t}", [P, n_rows], F32)) for t in range(TILES)]
        rot_ps = [ctx.enter_context(nc.psum_tensor(f"rot_ps{t}", [P, n_rows], F32)) for t in range(ROT)]

        u_raw = sem("u_raw")
        u_full = sem("u_full")
        unit_ready = sem("unit_ready")
        off_copied = sem("off_copied")
        exp_done = sem("exp_done")
        hw_hi_done = sem("hw_hi_done")
        hw_lo_done = sem("hw_lo_done")
        x_shift_done = sem("x_shift_done")
        x_norm_act_done = sem("x_norm_act_done")
        x_norm_dve_done = sem("x_norm_dve_done")
        ht_hi_done = sem("ht_hi_done")
        et_hi_done = sem("et_hi_done")
        max_done = sem("max_done")
        masked = sem("masked")
        diag_done = sem("diag_done")
        recip_done = sem("recip_done")
        bank_freed = sem("bank_freed")
        stats_done = sem("stats_done")
        aggr_done = sem("aggr_done")
        var_done = sem("var_done")
        final_done = sem("final_done")
        dg_done = sem("dg_done")
        centred = sem("centred")
        scale_done = sem("scale_done")
        affine_done = sem("affine_done")
        rstd_done = sem("rstd_done")
        x_rstd_done = sem("x_rstd_done")
        x_stats_done = sem("x_stats_done")
        x_loaded = [sem(f"x_loaded_{g}") for g in "ab"]
        x_first = [sem(f"x_first_{t}") for t in range(TILES)]
        adj_loaded = [sem(f"adj_loaded_{g}") for g in "ab"]
        out_stored = sem("out_stored")
        consts = sem("consts")
        vec_loaded = sem("vec_loaded")
        vec_split = sem("vec_split")
        pick_done = sem("pick_done")
        w_loaded = [sem(f"w_loaded_{c}") for c in range(layers * KB)]
        vec_spread = sem("vec_spread")
        vec_copied = [sem("vec_copied_act"), sem("vec_copied_dve")]
        w_hi_done = sem("w_hi_done")
        w_lo0_done = sem("w_lo0_done")
        w_lo1_done = sem("w_lo1_done")

        XS = 2 * TILES + 1
        X_ACT, X_DVE = 2, TILES - 2

        def bank(s, unit):
            return rot_ps[(UNITS * s + unit) % ROT]

        def value(per_step, it, s, count):
            return it * (STEPS * per_step) + (per_step * s + count)

        def ready(it, s, unit):
            return value(UNITS, it, s, KB + unit + 1)

        def freed(it, s, unit):
            return value(UNITS, it, s, FREED0 + unit + 1)

        def all_pairs(eng, body):
            body(0, True, False)
            with eng.Fori(1, pairs - 1) as it:
                body(it, False, False)
            body(pairs - 1, False, True)

        def rows(dram, graph):
            return dram[graph].rearrange("(t p) n -> p t n", p=P)

        w_parts = [wl_t, wr_t, ws_t]
        chunks = [(layer, kb) for layer in range(layers) for kb in range(KB)]

        def flat(tile, lo, hi):
            return tile[:, :, :].rearrange("p t n -> p (t n)")[:, lo:hi]

        w_stages = [w_stage[:, 0, :], w_stage[:, 1, :], flat(z, 0, 3 * dim),
                    w_stage[:, 0, :], w_stage[:, 1, :], w_stage[:, 0, :]]
        sources = [bl, br, bs, ln_w, ln_b]
        n_vec = layers * len(sources)
        vec_rows = e_sb[0:n_vec, 0, 0:dim]
        vec_hi = hw_hi[0:n_vec, 0, 0:dim]
        vec_lo = hw_lo[0:n_vec, 0, 0:dim]
        pick_row = (ht_hi[0:n_vec, 1, :, :].rearrange("p k n -> p (k n)")[:, 0:n_vec * P]
                    .rearrange("p (n i) -> p n i", i=P))
        vec_tiles = ([bias[:, layer, n, :] for n in range(3) for layer in range(layers)]
                     + [tile[:, layer, :] for tile in (gamma, beta) for layer in range(layers)])
        vec_banks = u_ps + u_ps + rot_ps[:n_vec - 2 * TILES]
        assert n_vec == 2 * TILES + 2

        block = ctx.enter_context(nc.Block())

        @block.sync
        def _(sp):
            def load_w(c):
                layer, kb = chunks[c]
                for n, part in enumerate(w_parts):
                    sp.dma_start(w_stages[c][:, n * dim:(n + 1) * dim],
                                 part[layer, kb * P:(kb + 1) * P, :]).then_inc(w_loaded[c], 16)

            for t in range(TILES):
                sp.dma_start(x_sb[0][:, t, :], rows(x, 0)[:, t, :]).then_inc(x_first[t], 16)
            for n, vec in enumerate(sources):
                sp.dma_start(vec_rows[n * layers:(n + 1) * layers, :], vec[:, :]).then_inc(vec_loaded, 16)
            for c in range(KB):
                load_w(c)
            sp.dma_start(adj_sb[0][:, :, :], rows(adj, 0)).then_inc(adj_loaded[0], 16)
            sp.dma_start(x_sb[1][:, :, :], rows(x, 1)).then_inc(x_loaded[1], 16)
            sp.wait_ge(w_lo0_done, 2)
            load_w(KB)
            load_w(KB + 1)
            sp.dma_start(adj_sb[1][:, :, :], rows(adj, 1)).then_inc(adj_loaded[1], 16)
            sp.wait_ge(w_lo1_done, 1)
            load_w(KB + 2)

            def pair(it, first, last):
                for g in range(2):
                    s = 2 + g
                    if not last:
                        sp.wait_ge(masked, value(TILES, it, s, TILES))
                        sp.dma_start(adj_sb[g][:, :, :], rows(adj, it * 2 + (2 + g))).then_inc(adj_loaded[g], 16)
                    for t in range(TILES):
                        sp.wait_ge(final_done, it * (2 * TILES) + (TILES * g + t + 1))
                        sp.dma_start(rows(out, it * 2 + g)[:, t, :], z[:, t, :]).then_inc(out_stored, 16)
                    if not last:
                        sp.dma_start(x_sb[g][:, :, :], rows(x, it * 2 + (2 + g))).then_inc(x_loaded[g], 16)

            all_pairs(sp, pair)
            sp.wait_ge(out_stored, 16 * (n_graphs * TILES + 1))

        @block.tensor
        def _(pe):
            def products(dst, pairs_of_operands, first=True, last=True):
                n = len(pairs_of_operands)
                for m, (a_hi, a_lo, b_hi, b_lo) in enumerate(pairs_of_operands):
                    pe.matmul(dst, a_hi, b_hi, start=first and m == 0, stop=False)
                    pe.matmul(dst, a_hi, b_lo, start=False, stop=False)
                    done = pe.matmul(dst, a_lo, b_hi, start=False, stop=last and m == n - 1)
                return done

            def spread(n):
                if TILES <= n < 2 * TILES:
                    pe.wait_ge(vec_copied[n % 2], (n - TILES) // 2 + 1)
                pe.matmul(vec_banks[n][:, 0:dim], pick_row[:, n, :], vec_hi, start=True, stop=False)
                pe.matmul(vec_banks[n][:, 0:dim], pick_row[:, n, :], vec_lo,
                          start=False, stop=True).then_inc(vec_spread, 1)

            pe.wait_ge(pick_done, 1)
            pe.wait_ge(vec_split, 2)
            for n in range(TILES):
                spread(n)
            pe.wait_ge(x_norm_dve_done, X_DVE)
            pe.wait_ge(x_norm_act_done, X_ACT)
            for db in range(KB):
                for t in range(TILES):
                    done = pe.transpose(rot_ps[(db - KB) % ROT][:, t * P:(t + 1) * P],
                                        x_norm[:, t, db * P:(db + 1) * P], ident[:, :])
                done.then_inc(unit_ready, 1)
            for n in range(TILES, n_vec):
                if n == n_vec - 1:
                    pe.wait_ge(bank_freed, CREDIT + 1)
                spread(n)
            pe.wait_ge(bank_freed, FREED0)

            def step(it, s, first, last):
                final = last and s == STEPS - 1
                order = ORDER_LAST if final else ORDER

                def unit(*what):
                    return order.index(what)

                cur, layer = s % 2, s // 2
                a_t = [ht_hi[:, cur], ht_lo[:, cur]]

                def project(t, n):
                    pe.wait_ge(bank_freed, freed(it, s, unit("P", t, n) - ROT))
                    lo, hi = t * P, (t + 1) * P
                    cols = slice(n * dim, (n + 1) * dim)
                    products(bank(s, unit("P", t, n))[:, 0:dim],
                             [(a_t[0][:, kb, lo:hi], a_t[1][:, kb, lo:hi],
                               w_hi[:, layer, kb, cols], w_lo[:, layer, kb, cols])
                              for kb in range(KB)]).then_inc(unit_ready, 1)

                def transpose_h(db):
                    src = z if s in (1, 2) else x_norm
                    pe.wait_ge(bank_freed, freed(it, s, unit("T", db) - ROT))
                    for t in range(TILES):
                        done = pe.transpose(bank(s, unit("T", db))[:, t * P:(t + 1) * P],
                                            src[:, t, db * P:(db + 1) * P], ident[:, :])
                    done.then_inc(unit_ready, 1)

                def transpose_e(i):
                    pe.wait_ge(masked, value(TILES, it, s, i + 1))
                    pe.wait_ge(bank_freed, freed(it, s, unit("E", i) - ROT))
                    for j in range(TILES):
                        done = pe.transpose(bank(s, unit("E", i))[:, j * P:(j + 1) * P],
                                            e_sb[:, i, j * P:(j + 1) * P], ident[:, :])
                    done.then_inc(unit_ready, 1)

                def attend(i):
                    pe.wait_ge(bank_freed, freed(it, s, max(unit("E", i), unit("C", i) - ROT)))
                    dst = bank(s, unit("C", i))[:, 0:dim]
                    for m, j in enumerate(j for j in range(TILES) if j != i):
                        if i == 0:
                            pe.wait_ge(hw_lo_done, value(TILES, it, s, j + 1))
                        cols = slice((j < i) * dim, ((j < i) + 1) * dim)
                        products(dst, [(et_hi[:, i % 2, j * P:(j + 1) * P], et_lo[:, i % 2, j * P:(j + 1) * P],
                                        hw_hi[:, j, cols], hw_lo[:, j, cols])], first=m == 0, last=False)
                    pe.wait_ge(dg_done, value(2 * TILES, it, s, 2 * (i + 1)))
                    products(dst, [(dg[:, i % 2, 0, n, :], dg[:, i % 2, 1, n, :],
                                    hw_hi[:, i, n * dim:(n + 1) * dim], hw_lo[:, i, n * dim:(n + 1) * dim])
                                   for n in range(2)], first=False).then_inc(unit_ready, 1)

                pe.wait_ge(bank_freed, value(UNITS, it, s, FREED0 + ORDER.index(("T", KB - 1)) + 1 - UNITS))
                for t in range(TILES):
                    if first and s == 0:
                        pe.wait_ge(vec_copied[t % 2], (TILES + t) // 2 + 1)
                    lo, hi = t * P, (t + 1) * P
                    left = U_FROM[t] * P
                    products(u_ps[t][:, left:n_rows],
                             [(a_t[0][:, kb, lo:hi], a_t[1][:, kb, lo:hi],
                               a_t[0][:, kb, left:n_rows], a_t[1][:, kb, left:n_rows])
                              for kb in range(KB)]).then_inc(u_raw, 1)
                if first and s == 0:
                    pe.wait_ge(vec_copied[0], n_vec // 2)
                    pe.wait_ge(vec_copied[1], n_vec // 2)
                    pe.wait_ge(w_lo0_done, KB)
                if first and s == 2:
                    pe.wait_ge(w_lo1_done, KB)
                project(0, 0)
                project(0, 1)
                for t in range(1, TILES):
                    if t < TILES - 1:
                        pe.wait_ge(off_copied, value(2, it, s, min(t + 1, 2)))
                    for above in range(U_FROM[t]):
                        at = off_at[above] + (t - above - 1) * P
                        done = pe.transpose(u_ps[t][:, above * P:(above + 1) * P],
                                            u_off[:, at:at + P], ident[:, :])
                    done.then_inc(u_full, 1)
                for what in order[2:]:
                    if what[0] == "P":
                        project(*what[1:])
                    elif what[0] == "T":
                        if what[1] == 0:
                            if s in (1, 2):
                                pe.wait_ge(affine_done, value(TILES, it, s, 0))
                            else:
                                nth = 2 if s == 0 else 3
                                pe.wait_ge(x_norm_dve_done, it * (2 * X_DVE) + nth * X_DVE)
                                pe.wait_ge(x_norm_act_done, it * (2 * X_ACT) + nth * X_ACT)
                        transpose_h(what[1])
                    elif what[0] == "E":
                        transpose_e(what[1])
                    else:
                        attend(what[1])

            all_pairs(pe, lambda it, first, last: [step(it, s, first, last) for s in range(STEPS)])

        @block.scalar
        def _(act):
            def x_normalise(count, g):
                act.wait_ge(x_shift_done, count)
                for t in range(X_ACT):
                    act.activation(x_norm[:, t, :], x_sb[g][:, t, :], ACT.Identity, bias=x_shift[:, t:t + 1],
                                   scale=x_rstd[:, t:t + 1]).then_inc(x_norm_act_done, 1)

            def split_ht(parity, banks):
                for db, (src, count) in enumerate(banks):
                    act.wait_ge(unit_ready, count)
                    act.activation(ht_hi[:, parity, db, :], src, ACT.Relu).then_inc(ht_hi_done, 1)

            def round_w(c):
                layer, kb = chunks[c]
                act.wait_ge(w_loaded[c], 16 * len(w_parts))
                act.activation(w_hi[:, layer, kb, :], w_stages[c], ACT.Copy).then_inc(w_hi_done, 1)

            def copy_vector(n):
                act.wait_ge(vec_spread, n + 1)
                act.activation(vec_tiles[n], vec_banks[n][:, 0:dim], ACT.Copy).then_inc(vec_copied[0], 1)

            act.wait_ge(vec_loaded, 16 * len(sources))
            act.activation(vec_hi, vec_rows, ACT.Copy).then_inc(vec_split, 1)
            x_normalise(1, 0)
            for n in range(0, TILES, 2):
                copy_vector(n)
            split_ht(0, [(rot_ps[(db - KB) % ROT][:, :], db + 1) for db in range(KB)])
            for n in range(TILES, n_vec, 2):
                copy_vector(n)
            for c in range(KB):
                round_w(c)

            def step(it, s, first, last):
                final = last and s == STEPS - 1
                order = ORDER_LAST if final else ORDER

                def unit(*what):
                    return order.index(what)

                def copy_off(t):
                    act.wait_ge(u_raw, value(TILES, it, s, t + 1))
                    width = (TILES - 1 - t) * P
                    act.activation(u_off[:, off_at[t]:off_at[t] + width], u_ps[t][:, (t + 1) * P:n_rows],
                                   ACT.Copy).then_inc(off_copied, 1)

                def exp(t):
                    act.wait_ge(max_done, value(TILES, it, s, t + 1))
                    act.activation(e_sb[:, t, :], u_ps[t][:, :], ACT.Exp, bias=neg_max[:, t:t + 1],
                                   scale=scale, accum_out=z_sum[:, t:t + 1]).then_inc(exp_done, 1)

                for t in range(2):
                    copy_off(t)
                for t in range(TILES):
                    exp(t)

                def split_proj(t):
                    act.wait_ge(bank_freed, freed(it, s, unit("P", t, 1)))
                    act.activation(hw_hi[:, t, :], proj[:, t % 2, :], ACT.Copy).then_inc(hw_hi_done, 1)

                def split_e(i):
                    act.wait_ge(unit_ready, ready(it, s, unit("E", i)))
                    act.activation(et_hi[:, i % 2, :], bank(s, unit("E", i))[:, :], ACT.Copy).then_inc(et_hi_done, 1)

                for t in range(TILES - 1):
                    split_proj(t)
                if s == 0:
                    x_normalise(it * 2 + 2, 1)
                elif s == STEPS - 1 and not last:
                    x_normalise(it * 2 + 3, 0)
                split_e(0)
                split_proj(TILES - 1)
                split_e(1)
                if order is ORDER:
                    split_ht(1 - s % 2, [(bank(s, unit("T", db))[:, :], ready(it, s, unit("T", db)))
                                         for db in range(KB)])
                split_e(2)
                split_e(3)
                if first and s == 0:
                    round_w(KB)
                    round_w(KB + 1)
                if first and s == 1:
                    round_w(KB + 2)

            all_pairs(act, lambda it, first, last: [step(it, s, first, last) for s in range(STEPS)])

        @block.vector
        def _(dve):
            def x_statistics(g, first=False):
                for t in range(TILES):
                    if first:
                        dve.wait_ge(x_first[t], 16)
                    dve.bn_stats(x_stats[:, t, :], x_sb[g][:, t, :]).then_inc(x_stats_done, 1)

            def x_variance(count):
                for t in range(TILES):
                    dve.bn_aggr(x_mv[:, t, :], x_stats[:, t, :]).then_inc(x_stats_done, 1)
                dve.wait_ge(x_stats_done, (count - 1) * XS + 2 * TILES)
                dve.tensor_scalar(x_var_eps[:, :], x_mv[:, :, 1], 1e-5, None, ALU.add).then_inc(x_stats_done, 1)

            def x_shift_of(count):
                dve.wait_ge(x_rstd_done, count)
                dve.scalar_tensor_tensor(out=x_shift[:, :], in0=x_mv[:, :, 0], scalar=-1.0, in1=x_rstd[:, :],
                                         op0=ALU.mult, op1=ALU.mult).then_inc(x_shift_done, 1)

            def x_normalise_rest(g):
                for t in range(X_ACT, TILES):
                    dve.tensor_scalar(x_norm[:, t, :], x_sb[g][:, t, :], x_rstd[:, t:t + 1], x_shift[:, t:t + 1],
                                      ALU.mult, ALU.add).then_inc(x_norm_dve_done, 1)

            def low_part(dst, src, hi):
                dve.tensor_tensor(dst, src, hi.bitcast(F32), ALU.subtract).then_inc(bank_freed, 1)

            def split_ht(parity, banks):
                for db, (src, count) in enumerate(banks):
                    dve.wait_ge(ht_hi_done, count)
                    dve.scalar_tensor_tensor(out=ht_lo[:, parity, db, :], in0=src, scalar=0.0,
                                             in1=ht_hi[:, parity, db, :].bitcast(F32), op0=ALU.max,
                                             op1=ALU.subtract).then_inc(bank_freed, 1)

            dve.memset(diag_junk[:, :, :], 0.0).then_inc(bank_freed, CREDIT)
            x_statistics(0, first=True)
            dve.wait_ge(x_stats_done, TILES)
            x_variance(1)
            dve.wait_ge(consts, 6)
            dve.tensor_copy(pick_row,
                            ident[0:n_vec, 0:n_vec].unsqueeze(2).to_broadcast([n_vec, n_vec, P])).then_inc(pick_done, 1)
            dve.wait_ge(vec_split, 1)
            dve.tensor_tensor(vec_lo, vec_rows, vec_hi.bitcast(F32), ALU.subtract).then_inc(vec_split, 1)
            x_shift_of(1)
            dve.wait_ge(x_shift_done, 1)
            x_normalise_rest(0)

            def copy_vector(n):
                dve.wait_ge(vec_spread, n + 1)
                dve.tensor_copy(vec_tiles[n], vec_banks[n][:, 0:dim]).then_inc(vec_copied[1], 1)

            for n in range(1, TILES, 2):
                copy_vector(n)
            split_ht(0, [(rot_ps[(db - KB) % ROT][:, :], db + 1) for db in range(KB)])
            for n in range(TILES + 1, n_vec, 2):
                copy_vector(n)
            for c in range(KB):
                dve.wait_ge(w_hi_done, c + 1)
                dve.tensor_tensor(w_lo[:, 0, c, :], w_stages[c], w_hi[:, 0, c, :].bitcast(F32),
                                  ALU.subtract).then_inc(w_lo0_done, 1)
            dve.wait_ge(vec_copied[0], n_vec // 2)
            dve.wait_ge(vec_copied[1], n_vec // 2)
            dve.wait_ge(bank_freed, CREDIT)

            def step(it, s, first, last):
                final = last and s == STEPS - 1
                order = ORDER_LAST if final else ORDER

                def unit(*what):
                    return order.index(what)

                g, layer = s % 2, s // 2

                def row_max(t):
                    if t == 0:
                        dve.wait_ge(off_copied, value(2, it, s, 1))
                    else:
                        dve.wait_ge(u_full, value(3, it, s, t))
                    dve.tensor_scalar(e_sb[:, t, :], u_ps[t][:, :], -scale, None, ALU.mult, ALU.min,
                                      accum_out=neg_max[:, t:t + 1]).then_inc(max_done, 1)

                def mask(t):
                    if t == 0:
                        dve.wait_ge(adj_loaded[g], it * 16 + 16)
                    dve.wait_ge(exp_done, value(TILES, it, s, t + 1))
                    dve.scalar_tensor_tensor(out=e_sb[:, t, :], in0=e_sb[:, t, :], scalar=1.0,
                                             in1=adj_sb[g][:, t, :], op0=ALU.mult, op1=ALU.mult,
                                             accum_out=e_sum[:, t:t + 1]).then_inc(masked, 1)

                def project(t, n):
                    dve.wait_ge(unit_ready, ready(it, s, unit("P", t, n)))
                    if n == 2:
                        dst = hs[:, t, :]
                    else:
                        if n == 0 and t >= 2:
                            dve.wait_ge(hw_lo_done, value(TILES, it, s, t - 1))
                        dst = proj[:, t % 2, n * dim:(n + 1) * dim]
                    dve.tensor_tensor(dst, bank(s, unit("P", t, n))[:, 0:dim], bias[:, layer, n, :],
                                      ALU.add).then_inc(bank_freed, 1)

                def diagonal(t):
                    dve.wait_ge(masked, value(TILES, it, s, t + 1))
                    dve.scalar_tensor_tensor(out=diag_junk[:, t, :], in0=e_sb[:, t, t * P:(t + 1) * P],
                                             scalar=1.0, in1=ident[:, :], op0=ALU.mult, op1=ALU.mult,
                                             accum_out=e_diag[:, t:t + 1]).then_inc(diag_done, 1)

                row_max(0)
                project(0, 0)
                project(0, 1)
                mask(0)
                for t in range(1, TILES):
                    row_max(t)
                project(0, 2)
                mask(1)
                project(1, 0)
                mask(2)
                project(1, 1)
                mask(3)
                project(1, 2)
                dve.wait_ge(masked, value(TILES, it, s, TILES))
                dve.scalar_tensor_tensor(out=den[:, :], in0=z_sum[:, :], scalar=1e-10, in1=e_sum[:, :],
                                         op0=ALU.mult, op1=ALU.add).then_inc(recip_done, 1)
                dve.wait_ge(recip_done, value(3, it, s, 1))
                dve.reciprocal(recip[:, :], den[:, :]).then_inc(recip_done, 1)
                dve.wait_ge(recip_done, value(3, it, s, 2))
                dve.tensor_tensor(recip_sq[:, :], recip[:, :], recip[:, :], ALU.mult).then_inc(recip_done, 1)
                count, x_from = {0: (it * 2 + 2, 1), 3: (it * 2 + 3, 0)}.get(s, (None, None))
                if order is not ORDER:
                    count = None
                if count is not None:
                    dve.wait_ge(x_loaded[x_from], it * 16 + 16)
                    x_statistics(x_from)
                project(2, 0)
                if count is not None:
                    dve.wait_ge(x_stats_done, (count - 1) * XS + TILES)
                project(2, 1)
                if count is not None:
                    x_variance(count)
                project(2, 2)
                if count is not None:
                    x_shift_of(count)
                project(3, 0)
                if count is not None:
                    dve.wait_ge(x_shift_done, count)
                    x_normalise_rest(x_from)

                def split_e(i):
                    dve.wait_ge(et_hi_done, value(TILES, it, s, i + 1))
                    low_part(et_lo[:, i % 2, :], bank(s, unit("E", i))[:, :], et_hi[:, i % 2, :])

                def variance(i):
                    dve.wait_ge(aggr_done, value(TILES, it, s, i + 1))
                    dve.tensor_scalar(var_eps[:, i:i + 1], mv[:, i, 1:2], recip_sq[:, i:i + 1], 1e-12,
                                      ALU.mult, ALU.add).then_inc(var_done, 1)

                def centre(i):
                    if i == 0 and s in (0, 3):
                        dve.wait_ge(out_stored, it * 128 + 16 * (1 + (s == 3) * TILES))
                    dve.scalar_tensor_tensor(out=z[:, i, :], in0=hs[:, i, :], scalar=mv[:, i, 0:1],
                                             in1=gamma[:, layer, :], op0=ALU.subtract,
                                             op1=ALU.mult).then_inc(centred, 1)

                def affine(t):
                    dve.wait_ge(centred, value(TILES, it, s, t + 1))
                    dve.scalar_tensor_tensor(out=z[:, t, :], in0=z[:, t, :], scalar=ln_scale[:, t:t + 1],
                                             in1=beta[:, layer, :], op0=ALU.mult,
                                             op1=ALU.add).then_inc(affine_done, 1)

                def add_x(t):
                    dve.wait_ge(affine_done, value(TILES, it, s, t + 1))
                    dve.scalar_tensor_tensor(out=z[:, t, :], in0=z[:, t, :], scalar=0.0,
                                             in1=x_sb[g][:, t, :], op0=ALU.max,
                                             op1=ALU.add).then_inc(final_done, 1)

                def close(i):
                    centre(i)
                    dve.wait_ge(rstd_done, value(1, it, s, i + 1))
                    dve.tensor_tensor(ln_scale[:, i:i + 1], rstd[:, i:i + 1], recip[:, i:i + 1],
                                      ALU.mult).then_inc(scale_done, 1)
                    dve.wait_ge(scale_done, value(1, it, s, i + 1))
                    affine(i)
                    add_x(i)

                def finish(i):
                    if i == 0:
                        for t in range(TILES):
                            diagonal(t)
                        dve.wait_ge(diag_done, value(TILES, it, s, TILES))
                    elif not final:
                        dve.wait_ge(stats_done, value(TILES, it, s, i))
                    dve.wait_ge(unit_ready, ready(it, s, unit("C", i)))
                    dve.scalar_tensor_tensor(out=hs[:, i, :], in0=hs[:, i, :], scalar=e_diag[:, i:i + 1],
                                             in1=bank(s, unit("C", i))[:, 0:dim], op0=ALU.mult,
                                             op1=ALU.add).then_inc(bank_freed, 1)
                    if i > 0 and not final:
                        dve.bn_aggr(mv[:, i - 1, :], stats[:, i - 1, :]).then_inc(aggr_done, 1)
                    dve.wait_ge(bank_freed, freed(it, s, unit("C", i)))
                    dve.bn_stats(stats[:, i, :], hs[:, i, :]).then_inc(stats_done, 1)
                    if final:
                        dve.wait_ge(stats_done, value(TILES, it, s, i + 1))
                        dve.bn_aggr(mv[:, i, :], stats[:, i, :]).then_inc(aggr_done, 1)
                        variance(i)
                    elif 0 < i < TILES - 1:
                        variance(i - 1)
                        centre(i - 1)

                for what in order[order.index(("P", 3, 1)):]:
                    if what[0] == "P":
                        project(*what[1:])
                    elif what == ("T", 0):
                        split_ht(1 - s % 2, [(bank(s, unit("T", db))[:, :], value(KB, it, s, KB + db + 1))
                                             for db in range(KB)])
                    elif what[0] == "E":
                        split_e(what[1])
                    elif what[0] == "C":
                        finish(what[1])
                    if final and what == ("E", 0):
                        dve.wait_ge(hw_hi_done, value(TILES, it, s, TILES))
                        dve.wait_ge(hw_lo_done, value(TILES, it, s, TILES - 1))
                        dve.tensor_tensor(hw_lo[:, TILES - 1, :], proj[:, (TILES - 1) % 2, :],
                                          hw_hi[:, TILES - 1, :].bitcast(F32), ALU.subtract).then_inc(hw_lo_done, 1)
                    if final and what == ("E", TILES - 1):
                        close(0)
                if final:
                    for t in range(1, TILES):
                        close(t)
                    return
                dve.wait_ge(stats_done, value(TILES, it, s, TILES))
                variance(TILES - 2)
                dve.bn_aggr(mv[:, TILES - 1, :], stats[:, TILES - 1, :]).then_inc(aggr_done, 1)
                variance(TILES - 1)
                centre(TILES - 2)
                centre(TILES - 1)
                dve.wait_ge(rstd_done, value(1, it, s, 1))
                dve.tensor_tensor(ln_scale[:, :], rstd[:, :], recip[:, :], ALU.mult).then_inc(scale_done, 1)
                dve.wait_ge(scale_done, value(1, it, s, 1))

                for t in range(TILES):
                    affine(t)
                    if layer == 1 and t > 0:
                        add_x(t - 1)
                if layer == 1:
                    add_x(TILES - 1)

            all_pairs(dve, lambda it, first, last: [step(it, s, first, last) for s in range(STEPS)])

        @block.gpsimd
        def _(pool):
            pool.memset(ident[:, :], 0.0).then_inc(consts, 1)
            pool.memset(tri[:, :, :], 1.0).then_inc(consts, 1)
            pool.memset(minus_half[:, :], -0.5).then_inc(consts, 1)
            pool.wait_ge(consts, 3)
            pool.affine_select(out=ident[:, :], in_=ident[:, :], compare_op=ALU.not_equal, fill=1.0,
                               base=0, pattern=[[-1, P]], channel_multiplier=1).then_inc(consts, 1)
            pool.affine_select(out=tri[:, 0, :], in_=tri[:, 0, :], compare_op=ALU.is_gt, fill=0.0,
                               base=0, pattern=[[-1, P]], channel_multiplier=1).then_inc(consts, 1)
            pool.affine_select(out=tri[:, 1, :], in_=tri[:, 1, :], compare_op=ALU.is_gt, fill=0.0,
                               base=0, pattern=[[1, P]], channel_multiplier=-1).then_inc(consts, 1)
            pool.memset(rstd[:, :], 0.0).then_inc(out_stored, 16)

            def x_rstd_of(count):
                pool.wait_ge(x_stats_done, count * XS)
                pool.tensor_tensor(x_rstd[:, :], x_var_eps[:, :], minus_half[:, :], ALU.pow).then_inc(x_rstd_done, 1)

            x_rstd_of(1)

            def split_w(c):
                pool.wait_ge(w_hi_done, c + 1)
                pool.tensor_tensor(w_lo[:, 1, c - KB, :], w_stages[c], w_hi[:, 1, c - KB, :].bitcast(F32),
                                   ALU.subtract).then_inc(w_lo1_done, 1)

            def step(it, s, first, last):
                final = last and s == STEPS - 1
                order = ORDER_LAST if final else ORDER

                def unit(*what):
                    return order.index(what)

                def split_proj(t):
                    pool.wait_ge(hw_hi_done, value(TILES, it, s, t + 1))
                    pool.tensor_tensor(hw_lo[:, t, :], proj[:, t % 2, :], hw_hi[:, t, :].bitcast(F32),
                                       ALU.subtract).then_inc(hw_lo_done, 1)

                def mask_diagonal(i):
                    for part, src in enumerate((et_hi, et_lo)):
                        if part == 0:
                            pool.wait_ge(et_hi_done, value(TILES, it, s, i + 1))
                        else:
                            pool.wait_ge(bank_freed, freed(it, s, unit("E", i)))
                        block_t = src[:, i % 2, i * P:(i + 1) * P].bitcast(F32)
                        pool.tensor_tensor(dg[:, i % 2, part, :, :], block_t.unsqueeze(1).to_broadcast([P, 2, P]),
                                           tri[:, :, :], ALU.mult).then_inc(dg_done, 1)

                def rstd_of(i):
                    pool.wait_ge(var_done, value(TILES, it, s, i + 1))
                    pool.tensor_tensor(rstd[:, i:i + 1], var_eps[:, i:i + 1], minus_half[:, i:i + 1],
                                       ALU.pow).then_inc(rstd_done, 1)

                split_proj(0)
                split_proj(1)
                if s == 0:
                    x_rstd_of(it * 2 + 2)
                elif s == STEPS - 1 and not last:
                    x_rstd_of(it * 2 + 3)
                split_proj(2)
                mask_diagonal(0)
                if not final:
                    split_proj(3)
                for i in range(1, TILES):
                    mask_diagonal(i)
                    if final and i > 1:
                        rstd_of(i - 2)
                if first and s == 0:
                    split_w(KB)
                    split_w(KB + 1)
                if first and s == 1:
                    split_w(KB + 2)
                if final:
                    rstd_of(TILES - 2)
                    rstd_of(TILES - 1)
                    return
                pool.wait_ge(var_done, value(TILES, it, s, TILES))
                pool.tensor_tensor(rstd[:, :], var_eps[:, :], minus_half[:, :], ALU.pow).then_inc(rstd_done, 1)

            all_pairs(pool, lambda it, first, last: [step(it, s, first, last) for s in range(STEPS)])


def kernel(x, adj, L0_gnn_Wl, L0_gnn_bl, L0_gnn_Ws, L0_gnn_bs, L0_gnn_Wr, L0_gnn_br, L0_gnn_ln_w, L0_gnn_ln_b):
    import numpy as np
    import concourse.bacc as bacc
    from concourse.bass_utils import run_bass_kernel_spmd

    nc = bacc.Bacc("TRN2", target_bir_lowering=False, num_devices=1)
    data = {
        "x": x, "adj": adj,
        "wl_t": np.transpose(L0_gnn_Wl, (0, 2, 1)), "bl": L0_gnn_bl,
        "ws_t": np.transpose(L0_gnn_Ws, (0, 2, 1)), "bs": L0_gnn_bs,
        "wr_t": np.transpose(L0_gnn_Wr, (0, 2, 1)), "br": L0_gnn_br,
        "ln_w": L0_gnn_ln_w, "ln_b": L0_gnn_ln_b,
    }
    arrays, args = {}, {}
    for name, value in data.items():
        a = np.ascontiguousarray(value)
        arrays[f"{name}_dram"] = a
        args[name] = nc.dram_tensor(f"{name}_dram", a.shape, mybir.dt.from_np(a.dtype), kind="ExternalInput").ap()
    args["out"] = nc.dram_tensor("out_dram", x.shape, F32, kind="ExternalOutput").ap()
    build_digcn(nc, **args)
    result = run_bass_kernel_spmd(nc, [arrays], core_ids=[0])
    return result.results[0]["out_dram"]
```
